# Optimizing a Trainium2 kernel written in Bass

```python
import numpy as np
import jax
import jax.numpy as jnp

def _softmax(x, axis=-1):
    return jax.nn.softmax(x, axis=axis)
def _gelu(x):
    return jax.nn.gelu(x, approximate=True)
def _silu(x):
    return jax.nn.silu(x)
def _sigmoid(x):
    return jax.nn.sigmoid(x)
def _layernorm(x, axis=-1, eps=1e-5):
    m = jnp.mean(x, axis=axis, keepdims=True)
    v = jnp.var(x, axis=axis, keepdims=True)
    return (x - m) / jnp.sqrt(v + eps)
def _scatter_add(tgt, idx, src, axis=0):
    return tgt.at[idx].add(src)
def _segment_sum(src, seg, n):
    return jax.ops.segment_sum(src, seg, n)

kernel_name = 'mk_adj_resnorm_d2_adj_128_ea5a1b'

def setup_inputs(seed: int = 0):
    np.random.seed(seed)
    _w = jnp.asarray
    def _rec_inputs():
        import jax
        import jax.numpy as jnp
        _gk = jax.random.key(seed)
        x = -0.000929 + 1 * jax.random.normal(jax.random.fold_in(_gk, 1), (8192, 128), jnp.float32)
        _w = (1.0 + jnp.arange(8192, dtype=jnp.float32)) ** -0.5
        _w = _w / _w.mean()
        _pij = jnp.clip(0.000488281 * _w[:, None] * _w[None, :], 0.0, 1.0)
        _a = jax.random.uniform(jax.random.fold_in(_gk, 2), (8192, 8192)) < _pij
        _a = jnp.logical_or(_a, jnp.eye(8192, dtype=bool))
        _af = _a.astype(jnp.float32)
        adj = _af
        return x, adj
    x, adj = _rec_inputs()
    def _L0_gnn_setup():
        import jax, jax.numpy as jnp
        import numpy as np
        N = 8192
        F_IN = 128
        F_OUT = 128
        BLOCK = 64

        def _graph_pool(out, adj):
            neg = jnp.asarray(jnp.finfo(out.dtype).min, out.dtype)

            def body(_, adj_blk):
                masked = jnp.where(adj_blk[:, :, None] != 0, out[None, :, :], neg)
                return (None, jnp.max(masked, axis=1))
            _, blocks = jax.lax.scan(body, None, adj.reshape(N // BLOCK, BLOCK, N))
            return blocks.reshape(N, out.shape[-1])
        key = jax.random.key(seed)
        k_in, k_adj, k_w, k_b = jax.random.split(key, 4)
        x = jax.random.normal(k_in, (N, F_IN), dtype=jnp.float32)
        adj = (jax.random.uniform(k_adj, (N, N)) < 0.01).astype(jnp.float32)
        adj = adj.at[jnp.arange(N), jnp.arange(N)].set(1.0)
        stdv = 1.0 / np.sqrt(F_OUT)
        weight = jax.random.uniform(k_w, (F_IN, F_OUT), minval=-stdv, maxval=stdv, dtype=jnp.float32)
        bias = jax.random.uniform(k_b, (F_OUT,), minval=-stdv, maxval=stdv, dtype=jnp.float32)
        return {'input': x, 'adj': adj, 'weight': weight, 'bias': bias}
    _L0_gnn_all = _L0_gnn_setup()
    _L0_gnn_in = {k: v for k, v in _L0_gnn_all.items() if k in ('weight', 'bias', )}
    del _L0_gnn_all

    def _L1_gnn_setup():
        import jax, jax.numpy as jnp
        import numpy as np
        N = 8192
        D = 128
        EPS = 1e-07
        NEG = -1000000000.0
        key = jax.random.key(seed)
        kx, ka, kb = jax.random.split(key, 3)
        x = jax.random.normal(kx, (N, D), dtype=jnp.float32)
        adj = jax.random.randint(ka, (N, N), 0, 2).astype(jnp.float32)
        adj = adj.at[jnp.arange(N), jnp.arange(N)].set(1.0)
        beta = jax.random.uniform(kb, (1,), dtype=jnp.float32)
        return {'x': x, 'adj': adj, 'beta': beta}
    _L1_gnn_all = _L1_gnn_setup()
    _L1_gnn_in = {k: v for k, v in _L1_gnn_all.items() if k in ('beta', )}
    del _L1_gnn_all

    return {
        "x": x,
        "adj": adj,
        "L0_gnn_weight": _L0_gnn_in["weight"],
        "L0_gnn_bias": _L0_gnn_in["bias"],
        "L1_gnn_beta": _L1_gnn_in["beta"],
    }

def reference(x, adj, L0_gnn_weight, L0_gnn_bias, L1_gnn_beta):
    import jax
    import jax.numpy as jnp
    def _L0_gnn_ref(input, adj, weight, bias):
        import jax, jax.numpy as jnp
        import numpy as np
        N = 8192
        F_IN = 128
        F_OUT = 128
        BLOCK = 64

        def _graph_pool(out, adj):
            neg = jnp.asarray(jnp.finfo(out.dtype).min, out.dtype)

            def body(_, adj_blk):
                masked = jnp.where(adj_blk[:, :, None] != 0, out[None, :, :], neg)
                return (None, jnp.max(masked, axis=1))
            _, blocks = jax.lax.scan(body, None, adj.reshape(N // BLOCK, BLOCK, N))
            return blocks.reshape(N, out.shape[-1])
        h = input @ weight
        out = jnp.maximum(adj @ h + bias, 0.0)
        return _graph_pool(out, adj)

    def _L1_gnn_ref(x, adj, beta):
        import jax, jax.numpy as jnp
        import numpy as np
        N = 8192
        D = 128
        EPS = 1e-07
        NEG = -1000000000.0
        norm2 = jnp.linalg.norm(x, axis=1, keepdims=True)
        cos = beta * (x @ x.T) / (norm2 @ norm2.T + EPS)
        masked = cos + (1.0 - adj) * NEG
        P = jax.nn.softmax(masked, axis=1)
        return P @ x

    x = _layernorm(x + _L0_gnn_ref(x, adj, L0_gnn_weight, L0_gnn_bias), axis=-1)
    x = _layernorm(x + _L1_gnn_ref(x, adj, L1_gnn_beta), axis=-1)
    return x


_drawn_inputs = setup_inputs


def setup_inputs(seed=0):
    import zlib

    import numpy as np

    out = dict(_drawn_inputs(seed))
    spreads = {}
    factors = {}
    for name, (base, spread) in spreads.items():
        noise = np.random.default_rng([zlib.crc32(name.encode()), seed]).standard_normal(out[name].shape)
        drawn = base * np.exp(spread * noise) if base else spread * noise
        out[name] = jnp.asarray(drawn.astype(out[name].dtype))
    for name, factor in factors.items():
        out[name] = (out[name] * factor).astype(out[name].dtype)
    return out
```

```python
import numpy as np
import concourse.bass as bass
from concourse import mybir
from contextlib import ExitStack


def adj_resnorm_program(nc, x, adj, weight, bias, beta, out):
    fp32, bf16 = mybir.dt.float32, mybir.dt.bfloat16
    u32, i32 = mybir.dt.uint32, mybir.dt.int32
    ALU = mybir.AluOpType
    ACT = mybir.ActivationFunctionType
    AX = mybir.AxisListType

    P = 128
    N, F = adj.shape[0], weight.shape[1]
    TILES = N // P
    SLICE = 512
    SLICES = N // SLICE
    PER = SLICE // P
    SUBS = 4
    SUBW = N // SUBS
    SPS = SUBW // SLICE
    LANES = (8, 8, 4, 2)
    PART_ROW = (0, 16, 32, 64)
    PARTS = len(LANES)
    ENTRIES = PARTS + TILES - 1
    PAIRS = TILES // 2
    COLS = 16
    GR = 16
    QD = 4
    RINGS = 16
    CREDIT = RINGS // 2
    TW = F + 4
    FLAT = ENTRIES * N + 4 * GR
    HC = 4
    CHUNKS = TILES // HC
    LNB = 8
    LN_EPS, COS_EPS = 1e-5, 1e-7

    HP = P // 2
    lists = [nc.dram_tensor(f"lists{i}", [HP, FLAT], u32, kind="Internal").ap() for i in range(2)]
    codes0 = nc.dram_tensor("codes0", [P, SLICE], fp32, kind="Internal").ap()
    tab_h = nc.dram_tensor("tab_h", [N + 1, F], fp32, kind="Internal").ap()
    tab0 = nc.dram_tensor("tab0", [N + 1, F], fp32, kind="Internal").ap()
    tab1 = nc.dram_tensor("tab1", [N + 1, TW], fp32, kind="Internal").ap()

    ctx = ExitStack()
    with ctx:
        def sb(name, shape, dt):
            return ctx.enter_context(nc.sbuf_tensor(name, shape, dt))

        def pb(name, shape, dt):
            return ctx.enter_context(nc.psum_tensor(name, shape, dt))

        def sem(name):
            return ctx.enter_context(nc.semaphore(name))

        big = sb("big", [P, 2 * SUBS * SUBW], fp32)
        row1 = big[:, 0:TILES * TW].rearrange("p (t w) -> p t w", w=TW)
        rows_sb = sb("rows_sb", [P, TILES, F], fp32)
        list_sb = sb("list_sb", [P, N + 3 * GR], u32)
        ofs = sb("ofs", [1, ENTRIES + 1], u32)
        got = sb("got", [P, 2 * RINGS + 1, TW], fp32)
        idx = [[sb(f"idx{i}_{h}", [P, GR], u32) for h in range(2)] for i in range(2)]
        stage = got[:].rearrange("p k w -> p (k w)")[:, 0:4 * HC * P].rearrange("p (b t f) -> p b t f", b=4, t=HC)
        squares = list_sb[:, 0:2 * LNB * F].bitcast(fp32).rearrange("p (k f) -> p k f", f=F)
        xs = [stage[:, i] for i in range(2)]
        xT = [stage[:, 2 + i] for i in range(2)]
        pow_id = sb("pow_id", [P, SLICES, P], bf16)
        neg_id = sb("neg_id", [P, P], bf16)
        ident = sb("ident", [P, P], fp32)
        to_row = sb("to_row", [P, PARTS, P], fp32)
        to_lane = sb("to_lane", [P, PARTS, P], fp32)
        bit = sb("bit", [P, SLICES], i32)
        base = sb("base", [P, SLICES], fp32)
        lane = sb("lane", [P, PARTS + 1], i32)
        first_col = sb("first_col", [P, PARTS + 1], fp32)
        code0 = sb("first_code", [P, SLICE], fp32)
        part_code = [sb(f"part_code{i}", [P, SLICE // LANES[i]], fp32) for i in range(PARTS)]
        is_set = sb("is_set", [P, SLICE], bf16)
        top = sb("top", [P, COLS], fp32)
        topi = sb("topi", [P, COLS], i32)
        col = sb("col", [P, COLS], u32)
        colf = sb("colf", [P, COLS], fp32)
        bits = sb("bits", [P, COLS, SLICES], i32)
        cand = sb("cand", [P, COLS, SLICES], fp32)
        best = sb("best", [P, 8], fp32)
        cnt = sb("cnt", [P, 32], fp32)
        cnt_t = sb("cnt_t", [P, 32], fp32)
        cnt_m = sb("cnt_m", [P, 32], fp32)
        cnt_u = sb("cnt_u", [P, 32], fp32)
        cnt_q = sb("cnt_q", [1, 4, 2], fp32)
        most = sb("most", [1, 2], fp32)
        mosti = sb("mosti", [1, 2], u32)
        length = sb("length", [1, 1], fp32)
        lengthi = sb("lengthi", [1, 1], i32)
        w_sb = sb("w_sb", [P, F], fp32)
        bias_sb = sb("bias_sb", [1, F], fp32)
        ones = sb("ones", [1, P], fp32)
        beta_sb = sb("beta_sb", [P, 1], fp32)
        shift = sb("shift", [P, 1], fp32)
        zeros = sb("zeros", [P, TW], fp32)
        zids = sb("zids", [P, 2 * GR], u32)
        most2 = sb("most2", [P, 2, F], fp32)
        pooled = sb("pooled", [P, F], fp32)
        pooledT = sb("pooledT", [P, P], fp32)
        ownc = [sb(f"ownc{i}", [P, TW], fp32) for i in range(2)]
        ownl = sb("ownl", [P, PARTS, TW], fp32)
        prod = sb("prod", [P, 2, F], fp32)
        dots = sb("dots", [P, 2], fp32)
        den = sb("den", [P, 2], fp32)
        score = sb("score", [P, 2], fp32)
        expo = sb("expo", [P, 2], fp32)
        diag = sb("diag", [P, 2, P], fp32)
        own_diag = sb("own_diag", [P, 2, P], fp32)
        stats = sb("stats", [P, 2 * LNB, 6], fp32)
        mv = sb("mv", [P, 2 * LNB, 2], fp32)
        nw = sb("nw", [P, 6, 2 * LNB], fp32)

        code = [pb(f"code_ps{i}", [P, SLICE], fp32) for i in range(2)]
        ps_t = pb("ps_t", [P, HC, P], fp32)
        ps_h = pb("ps_h", [P, HC, F], fp32)
        agg = [pb(f"agg{i}", [P, F], fp32) for i in range(2)]
        wsum = [pb(f"wsum{i}", [P, TW], fp32) for i in range(2)]

        consts = sem("consts")
        params = sem("params")
        loaded = sem("loaded")
        x_in = [sem(f"x_in{i}") for i in range(2)]
        x_turned = sem("x_turned")
        xT_copied = sem("xT_copied")
        h_done = sem("h_done")
        h_copied = sem("h_copied")
        h_saved = sem("h_saved")
        adj_in = [sem(f"adj_in{i}") for i in range(2 * SUBS)]
        adj_used = sem("adj_used")
        code_ready = [sem(f"code_ready{i}") for i in range(2)]
        code_used = [sem(f"code_used{i}") for i in range(2)]
        code0_ready = sem("code0_ready")
        code0_saved = sem("code0_saved")
        part_in = sem("part_in")
        list_ready = sem("list_ready")
        list_saving = sem("list_saving")
        list_saved = sem("list_saved")
        ends_saved = sem("ends_saved")
        SUMS, MAXIMA, ATTEND = range(3)
        idx_in = [[[sem(f"idx_in{w}_{i}_{h}") for h in range(2)] for i in range(2)] for w in range(3)]
        quad_in = [[sem(f"quad_in{w}_{i}") for i in range(2)] for w in range(3)]
        landed = [sem(f"landed{w}") for w in range(3)]
        used = [sem(f"used{w}") for w in range(3)]
        agg_done = [sem(f"agg_done{i}") for i in range(2)]
        relu_done = [sem(f"relu_done{i}") for i in range(2)]
        tab0_saved = sem("tab0_saved")
        x_again = sem("x_again")
        part_done = sem("part_done")
        part_turned = sem("part_turned")
        pooledT_ready = sem("pooledT_ready")
        pooledT_turned = sem("pooledT_turned")
        block1_done = sem("block1_done")
        tab1_saved = sem("tab1_saved")
        ownl_done = sem("ownl_done")
        own_ready = sem("own_ready")
        score_ready = sem("score_ready")
        score_used = sem("score_used")
        diag_ready = sem("diag_ready")
        diag_used = sem("diag_used")
        sum_done = sem("sum_done")
        sum_used = sem("sum_used")
        block2_done = sem("block2_done")
        out_saved = sem("out_saved")
        zeros_saved = sem("zeros_saved")

        block = ctx.enter_context(nc.Block())
        CONSTS = 8 + 2 + 3 * SLICES + 4 * PARTS + PARTS + 1

        class Count:

            def __init__(self, e, name):
                self.e, self.r = e, e.alloc_register(name)
                e.reg_mov(self.r, 0)

            def value(self, most=1 << 22):
                return self.e.snap(self.r, min_val=0, max_val=most)

            def set(self, v):
                self.e.reg_mov(self.r, v)

            def add(self, n=1):
                self.e.reg_add(self.r, self.r, n)

        def within(v, least, most, why="slots lie within the lists at their longest"):
            return nc.s_assert_within(v, least, most, skip_runtime_bounds_check_because=why)

        def end_of(e, entry):
            return e.value_load(ofs[0:1, entry + 1:entry + 2] if isinstance(entry, int)
                                else ofs[0:1, bass.ds(entry + 1, 1)], min_val=2, max_val=FLAT - 4 * GR)

        def at(buf, t):
            return buf[:, t, :] if isinstance(t, int) else buf[:, bass.ds(t, 1), :].rearrange("p a f -> p (a f)")

        def rows(table, t, ahead, tiles=1):
            if isinstance(t, int):
                return table[t * P + ahead:(t + tiles) * P + ahead, :]
            return table[bass.ds(t * P + ahead, tiles * P), :]

        ids_at = {}

        def load_ids(e, which, pa, start, n, first=True, others=True, told=None):
            ahead, from_ = ids_at[e]

            def half(q, h, first):
                ahead.set(start + q + h * GR)
                if not first:
                    e.wait_ge(used[which], (start + q) // 2 + h * (GR // 2))
                from_.set(ahead.value())
                begin = from_.value(FLAT - 2 * GR)
                for part in range(2):
                    e.dma_start(idx[pa][h][part * HP:(part + 1) * HP, :],
                                lists[part][:, bass.ds(begin, GR)]).then_inc(idx_in[which][pa][h], 16)
                if told:
                    told[pa][h].add()

            if first:
                half(0, 0, True)
                with e.If(n > GR):
                    half(0, 1, True)
                e.nop()
            if others:
                with e.If(n > 2 * GR):
                    with e.Fori(2 * GR, n, 2 * GR) as q:
                        half(q, 0, False)
                        with e.If(n > q + GR):
                            half(q, 1, False)
                        e.nop()
                    e.nop()
                e.nop()

        @block.sync
        def _(sp):
            sp.dma_start(w_sb[:], weight).then_inc(loaded, 16)
            sp.dma_start(bias_sb[:], bias.rearrange("(a f) -> a f", a=1)).then_inc(loaded, 16)
            sp.dma_start(beta_sb[:], beta.rearrange("(a f) -> a f", a=1).to_broadcast([P, 1])).then_inc(loaded, 16)

            def load_tile(t, bank, j):
                for s in range(SUBS):
                    i = bank * SUBS + s
                    if not isinstance(j, int):
                        sp.wait_ge(adj_used, (j - 1) * 2 * SUBS + i + 1)
                    sp.dma_start(big[:, i * SUBW:(i + 1) * SUBW],
                                 rows(adj, t, 0)[:, s * SUBW:(s + 1) * SUBW]).then_inc(adj_in[i], 16)

            load_tile(0, 0, 0)
            load_tile(TILES - 1, 1, 0)
            back = Count(sp, "sp_back")
            back.set(TILES - 1)
            with sp.Fori(1, PAIRS) as j:
                load_tile(j, 0, j)
                back.add(-1)
                load_tile(back.value(TILES - 1), 1, j)

            ids_at[sp] = (Count(sp, "sp_ahead"), Count(sp, "sp_from"))
            sp.wait_ge(adj_used, TILES * SUBS)
            n = TILES // 4
            for c in range(4):
                sp.dma_start(row1[:, c * n:(c + 1) * n, 0:F], x[c * n * P:(c + 1) * n * P, :]
                             .rearrange("(t p) f -> p t f", p=P)).then_inc(x_again, 16)
            sp.wait_ge(list_ready, ENTRIES)
            total = end_of(sp, ENTRIES - 1)
            sp.wait_ge(ends_saved, 32)
            for i in range(2):
                sp.wait_ge(agg_done[i], PAIRS)
            load_ids(sp, MAXIMA, 0, 0, total)
            sp.wait_ge(block1_done, PAIRS // LNB)
            load_ids(sp, ATTEND, 0, 0, total)
            sp.wait_ge(out_saved, 2 * 16 * PAIRS // LNB)

        @block.gpsimd
        def _(pool):
            for m in (ident, pow_id, neg_id, zeros, zids):
                pool.memset(m[:], 0.0 if m is not zids else 0).then_inc(consts, 1)
            for m in (ones, to_row, to_lane):
                pool.memset(m[:], 1.0).then_inc(consts, 1)
            pool.wait_ge(consts, 8)
            for m, fill in ((ident, 1.0), (neg_id, -1.0)):
                pool.affine_select(out=m[:], in_=m[:], compare_op=ALU.not_equal, fill=fill, base=0,
                                   pattern=[[-1, P]], channel_multiplier=1).then_inc(consts, 1)
            for s in range(SLICES):
                pool.affine_select(out=pow_id[:, s, :], in_=pow_id[:, s, :], compare_op=ALU.not_equal,
                                   fill=float(1 << s), base=0, pattern=[[-1, P]],
                                   channel_multiplier=1).then_inc(consts, 1)
                pool.memset(bit[:, s:s + 1], 1 << s).then_inc(consts, 1)
                pool.memset(base[:, s:s + 1], float(s * SLICE + 1)).then_inc(consts, 1)
            for p in range(PARTS + 1):
                pool.iota(lane[:, p:p + 1], pattern=[[0, 1]], base=0, channel_multiplier=1).then_inc(consts, 1)
            for sign in (1, -1):
                for p, (n, r) in enumerate(zip(LANES, PART_ROW)):
                    b = n * r if sign > 0 else n - 1 - n * r
                    pool.affine_select(out=to_row[:, p, :], in_=to_row[:, p, :], compare_op=ALU.is_ge, fill=0.0,
                                       base=b, pattern=[[-sign * n, P]], channel_multiplier=sign).then_inc(consts, 1)
                    pool.affine_select(out=to_lane[:, p, :], in_=to_lane[:, p, :], compare_op=ALU.is_ge, fill=0.0,
                                       base=b, pattern=[[sign, P]], channel_multiplier=-sign * n).then_inc(consts, 1)
                if sign > 0:
                    pool.wait_ge(consts, CONSTS - 2 * PARTS)

            issued = [Count(pool, f"issued{i}") for i in range(2)]
            taken = [[Count(pool, f"taken{i}_{h}") for h in range(2)] for i in range(2)]

            def landed_so_far(which, i):
                pool.wait_ge(quad_in[which][(i + 1) % 2], issued[(i + 1) % 2].value() * 64)
                pool.nop().then_inc(landed[which], 1)

            def gather(which, pa, table, width, start, n, q, first, whole):
                def quad(i):
                    h, k0 = i // 4, i % 4 * QD
                    if i % 4 == 0:
                        taken[pa][h].add()
                        pool.wait_ge(idx_in[which][pa][h], taken[pa][h].value() * 32)
                    if not first or i >= 4:
                        pool.wait_ge(used[which], (start + q) // 2 + 2 * i + 2)
                    issued[i % 2].add()
                    for k in range(k0, k0 + QD):
                        pool.indirect_dma_start(
                            out=got[:, pa * RINGS + k, 0:width], out_offset=None, in_=table,
                            in_offset=bass.IndirectOffsetOnAxis(ap=idx[pa][h][:, k:k + 1], axis=0),
                        ).then_inc(quad_in[which][i % 2], 16)
                    landed_so_far(which, i)
                    if i + 1 < 8:
                        if whole:
                            quad(i + 1)
                        else:
                            with pool.If(n > q + QD * (i + 1)):
                                quad(i + 1)
                            pool.nop()

                quad(0)

            def all_landed(which):
                for i in range(2):
                    pool.wait_ge(quad_in[which][i], issued[i].value() * 64)
                pool.nop().then_inc(landed[which], 1)

            start, before = Count(pool, "pool_start"), Count(pool, "pool_before")
            pool.wait_ge(h_saved, 16 * CHUNKS)
            pool.wait_ge(zeros_saved, 16 * 3)

            def sums(last_entry, entries, pa):
                pool.wait_ge(list_ready, entries)
                end = end_of(pool, last_entry)
                s = start.value(FLAT - 4 * GR)
                n = within(end - s, 4, FLAT)
                pool.wait_ge(used[SUMS], before.value() // 2 + CREDIT)
                gather(SUMS, pa, tab_h, F, s, n, 0, True, False)
                with pool.If(n > 32):
                    with pool.Fori(32, n, 32) as q:
                        gather(SUMS, pa, tab_h, F, s, n, q, False, False)
                    pool.nop()
                pool.nop()
                before.set(s)
                start.set(end)
                all_landed(SUMS)

            sums(PARTS, PARTS + 1, 0)
            sums(PARTS + 2, PARTS + 3, 1)
            with pool.Fori(1, PAIRS // 2) as v:
                for pa in range(2):
                    last = v * 4 + 2 * pa + PARTS
                    sums(last, last + 1, pa)

            total = end_of(pool, ENTRIES - 1)
            for which, saved, value, table, width in ((MAXIMA, tab0_saved, 16 * TILES, tab0, F),
                                                      (ATTEND, tab1_saved, 32 * PAIRS // LNB, tab1, TW)):
                for c in (*issued, *taken[0]):
                    c.set(0)
                pool.wait_ge(saved, value)
                gather(which, 0, table, width, 0, total, 0, True, True)
                with pool.Fori(32, total - 31, 32) as q:
                    gather(which, 0, table, width, 0, total, q, False, True)
                rest = within(total // 32 * 32, 32, FLAT)
                with pool.If(total > rest):
                    gather(which, 0, table, width, 0, total, rest, False, False)
                pool.nop()
                all_landed(which)

        @block.tensor
        def _(pe):
            pe.wait_ge(consts, CONSTS)
            pe.wait_ge(loaded, 48)
            for w in (SUMS, ATTEND):
                for _ in range(CREDIT):
                    pe.nop().then_inc(used[w], 1)
            pe.nop().then_inc(diag_used, 1)

            def codes(bank, j, c, s):
                for sub in range(SUBS):
                    i = bank * SUBS + sub
                    pe.wait_ge(adj_in[i], j * 16 + 16)
                    high = big[:, i * SUBW:(i + 1) * SUBW].bitcast(bf16)
                    for k in range(SPS):
                        mm = pe.matmul(code[bank][:], pow_id[:, sub * SPS + k, :],
                                       high[:, 2 * SLICE * k + 1:2 * SLICE * (k + 1):2],
                                       start=(sub == 0 and k == 0), stop=(sub == SUBS - 1 and k == SPS - 1))
                    mm.then_inc(adj_used, 1)
                pe.matmul(code[bank][:, c * P:(c + 1) * P], at(pow_id, s), neg_id[:],
                          start=False, stop=True, skip_group_check=True).then_inc(code_ready[bank], 1)

            codes(0, 0, 0, 0)

            def turn(c, i):
                pe.wait_ge(x_in[i], c // 2 * 16 + 16)
                if not (isinstance(c, int) and c == 0):
                    pe.wait_ge(xT_copied, c)
                for k in range(HC):
                    mm = pe.transpose(ps_t[:, k, :], xs[i][:, k, :], ident[:])
                mm.then_inc(x_turned, 1)

            def times_w(c, i):
                pe.wait_ge(xT_copied, c + 1)
                if not (isinstance(c, int) and c == 0):
                    pe.wait_ge(h_copied, c)
                for k in range(HC):
                    mm = pe.matmul(ps_h[:, k, :], xT[i][:, k, :], w_sb[:], start=True, stop=True)
                mm.then_inc(h_done, 1)

            turn(0, 0)
            turn(1, 1)
            times_w(0, 0)
            with pe.Fori(1, CHUNKS // 2) as v:
                for i in range(2):
                    turn(v * 2 + i, i)
                    times_w(v * 2 + i - 1, 1 - i)
            times_w(CHUNKS - 1, 1)

            end, quads, slots = Count(pe, "pe_end"), Count(pe, "pe_quads"), Count(pe, "pe_slots")

            def add_neighbours(entry, pa, bank, lhsT):
                pe.wait_ge(list_ready, entry + 1)
                until = end_of(pe, entry)
                with pe.Fori(end.value(FLAT - 4 * GR), until, 2):
                    pe.wait_ge(landed[SUMS], slots.value() // QD + quads.value() + 2)
                    k = slots.value() % RINGS + pa * RINGS
                    pe.matmul(agg[bank][:], lhsT, at(got, k)[:, 0:F], start=False, stop=False, skip_group_check=True)
                    pe.matmul(agg[bank][:], lhsT, at(got, k + 1)[:, 0:F], start=False, stop=False,
                              skip_group_check=True).then_inc(used[SUMS], 1)
                    slots.add(2)
                end.set(until)

            def aggregate(t, bank, j, pa, entry):
                if not isinstance(j, int):
                    pe.wait_ge(relu_done[bank], j)
                elif j > 0:
                    pe.wait_ge(relu_done[bank], j)
                else:
                    pe.wait_ge(h_copied, CHUNKS)
                pe.matmul(agg[bank][:], ones[:], bias_sb[:], start=True, stop=False, skip_group_check=True)
                pe.matmul(agg[bank][:], ident[:], at(rows_sb, t), start=False, stop=False, skip_group_check=True)
                if isinstance(j, int) and j == 0 and bank == 0:
                    for p in range(PARTS):
                        add_neighbours(p, pa, bank, to_row[:, p, :])
                else:
                    add_neighbours(entry, pa, bank, ident[:])
                pe.drain().then_inc(agg_done[bank], 1)
                if bank == 1:
                    quads.add((slots.value() + 3) // 4 + 1)
                    slots.set(0)

            codes(1, 0, PER - 1, SLICES - 1)

            def step(v, b, sums=True):
                j = v * PER + b
                pa = b % 2
                pe.wait_ge(code_used[0], j)
                codes(0, j, b, v)
                if sums:
                    aggregate(j - 2, 0, j - 2, pa, (j - 2) * 2 + PARTS - 1)
                pe.wait_ge(code_used[1], j)
                codes(1, j, PER - 1 - b, SLICES - 1 - v)
                if sums:
                    aggregate(TILES + 1 - j, 1, j - 2, pa, (j - 2) * 2 + PARTS)

            for b in range(1, PER):
                step(0, b, b > 1)
            with pe.Fori(1, PAIRS // PER) as v:
                for b in range(PER):
                    step(v, b)
            for j in (PAIRS - 2, PAIRS - 1):
                aggregate(j, 0, j, j % 2, j * 2 + PARTS - 1)
                aggregate(TILES - 1 - j, 1, j, j % 2, j * 2 + PARTS)

            for p in range(PARTS):
                pe.wait_ge(part_done, p + 1)
                pe.transpose(ps_t[:, 0, :], pooled[:], ident[:]).then_inc(part_turned, 1)
            pe.wait_ge(pooledT_ready, 1)
            pe.transpose(ps_t[:, 1, :], pooledT[:], ident[:]).then_inc(pooledT_turned, 1)

            pe.wait_ge(block1_done, PAIRS // LNB)
            for p in range(PARTS):
                mm = pe.matmul(ps_h[:, p, :], to_lane[:, p, :], row1[:, 0, 0:F], start=True, stop=True)
                mm = pe.matmul(ps_t[:, p, 0:TW - F], to_lane[:, p, :], row1[:, 0, F:TW], start=True, stop=True)
            mm.then_inc(ownl_done, 1)
            end.set(0)
            place, first, second = Count(pe, "pe_place"), Count(pe, "pe_first"), Count(pe, "pe_second")

            def weighted(bank, weights, values, start=False):
                return pe.matmul(wsum[bank][:, 0:F + 2], weights, values, start=start, stop=False,
                                 skip_group_check=True)

            def attend(bank, j, entry):
                if not (isinstance(j, int) and j == 0):
                    pe.wait_ge(sum_used, j * 2 + bank - 1)
                pe.wait_ge(own_ready, j * 2 + bank + 1)
                weighted(bank, own_diag[:, bank, :], ownc[bank][:, 0:F + 2], True)
                entries = range(PARTS) if isinstance(j, int) and j == 0 and bank == 0 else [entry]
                for e in entries:
                    until = end_of(pe, e)
                    with pe.Fori(end.value(FLAT - 4 * GR), until, 2) as s:
                        place.set(s % RINGS)
                        first.set(s + 1)
                        second.set(s + 2)
                        pe.wait_ge(diag_ready, first.value())
                        weighted(bank, diag[:, 0, :], at(got, place.value(RINGS - 2))[:, 0:F + 2]).then_inc(diag_used, 1)
                        pe.wait_ge(diag_ready, second.value())
                        weighted(bank, diag[:, 1, :], at(got, place.value(RINGS - 2) + 1)[:, 0:F + 2]
                                 ).then_inc(used[ATTEND], 1)
                    end.set(until)
                pe.drain().then_inc(sum_done, 1)

            attend(0, 0, None)
            attend(1, 0, PARTS)
            with pe.Fori(1, PAIRS) as j:
                attend(0, j, j * 2 + PARTS - 1)
                attend(1, j, j * 2 + PARTS)

        @block.scalar
        def _(act):
            def load_x(c, i):
                act.dma_start(xs[i], (x[c * HC * P:(c + 1) * HC * P, :] if isinstance(c, int)
                                      else x[bass.ds(c * (HC * P), HC * P), :])
                              .rearrange("(t p) f -> p t f", p=P)).then_inc(x_in[i], 16)

            def copy_xT(c, i):
                act.wait_ge(x_turned, c + 1)
                act.activation(xT[i], ps_t[:], ACT.Copy).then_inc(xT_copied, 1)

            def copy_h(c):
                act.wait_ge(h_done, c + 1)
                dst = rows_sb[:, c * HC:(c + 1) * HC, :] if isinstance(c, int) else rows_sb[:, bass.ds(c * HC, HC), :]
                act.activation(dst, ps_h[:], ACT.Copy).then_inc(h_copied, 1)
                act.wait_ge(h_copied, c + 1)
                act.dma_start(rows(tab_h, c * HC, 1, HC).rearrange("(t p) f -> p t f", p=P), dst
                              ).then_inc(h_saved, 16)

            load_x(0, 0)
            load_x(1, 1)
            act.wait_ge(consts, CONSTS)
            for table in (tab_h, tab0, tab1):
                act.dma_start(table[0:1, :], zeros[0:1, 0:table.shape[1]]).then_inc(zeros_saved, 16)

            act.wait_ge(code_ready[0], 1)
            act.activation(code0[:], code[0][:], ACT.Copy).then_inc(code_used[0], 1)
            act.wait_ge(code_used[0], 1)
            act.dma_start(codes0, code0[:]).then_inc(code0_saved, 16)
            act.wait_ge(code0_saved, 16)
            for p, (n, r) in enumerate(zip(LANES, PART_ROW)):
                act.dma_start(part_code[p][:], codes0[r:r + P // n, :].rearrange("r (l w) -> (r l) w", l=n)
                              ).then_inc(part_in, 16)

            copy_xT(0, 0)
            load_x(2, 0)
            copy_xT(1, 1)
            load_x(3, 1)
            copy_h(0)
            with act.Fori(1, CHUNKS // 2 - 1) as v:
                for i in range(2):
                    c = v * 2 + i
                    copy_xT(c, i)
                    load_x(c + 2, i)
                    copy_h(c - 1)
            for c in (CHUNKS - 2, CHUNKS - 1):
                copy_xT(c, c % 2)
                copy_h(c - 1)
            copy_h(CHUNKS - 1)

            saves = Count(act, "act_saves")
            ids_at[act] = (Count(act, "act_ahead"), Count(act, "act_from"))
            start, end = Count(act, "act_start"), Count(act, "act_end")
            first = [Count(act, f"act_first{i}") for i in range(2)]
            told = [[Count(act, f"act_told{i}_{h}") for h in range(2)] for i in range(2)]
            act.nop().then_inc(list_saved, 1)

            def save_list(entry, loads=()):
                act.wait_ge(list_ready, entry + 1)
                until = end_of(act, entry)
                begin = end.value(FLAT - 4 * GR)
                n = within(until - begin, 2, N)
                for i, h in loads:
                    act.wait_ge(idx_in[SUMS][i][h], told[i][h].value() * 32)
                for part in range(2):
                    act.dma_start(lists[part][:, bass.ds(begin, 2 * GR)],
                                  list_sb[part * HP:(part + 1) * HP, 0:2 * GR]).then_inc(list_saving, 16)
                saves.add()
                with act.If(n > GR):
                    with act.Fori(2 * GR, n + GR, GR) as q:
                        to = within(begin + q, 0, FLAT - 2 * GR)
                        for part in range(2):
                            act.dma_start(lists[part][:, bass.ds(to, GR)],
                                          list_sb[part * HP:(part + 1) * HP, bass.ds(q, GR)]).then_inc(list_saving, 16)
                        saves.add()
                    act.nop()
                act.nop()
                act.wait_ge(list_saving, saves.value() * 32)
                act.nop().then_inc(list_saved, 1)
                end.set(until)

            def first_ids(pa):
                act.wait_ge(used[SUMS], first[1 - pa].value() // 2 + CREDIT)
                begin, until = start.value(FLAT - 4 * GR), end.value(FLAT - 4 * GR)
                load_ids(act, SUMS, pa, begin, within(until - begin, 4, FLAT), others=False, told=told)
                first[pa].set(begin)
                start.set(until)

            def other_ids(pa):
                begin, until = first[pa].value(FLAT - 4 * GR), first[1 - pa].value(FLAT - 4 * GR)
                load_ids(act, SUMS, pa, begin, within(until - begin, 4, FLAT), first=False, told=told)

            def relu(t, bank, j):
                act.wait_ge(agg_done[bank], j + 1)
                act.activation(at(rows_sb, t), agg[bank][:], ACT.Relu).then_inc(relu_done[bank], 1)
                act.wait_ge(relu_done[bank], j + 1)
                act.dma_start(rows(tab0, t, 1), at(rows_sb, t)).then_inc(tab0_saved, 16)

            for p in range(PARTS):
                save_list(p)
            save_list(PARTS)
            first_ids(0)

            def relus(j):
                relu(j, 0, j)
                relu(TILES - 1 - j, 1, j)

            def step(j, pa, sums=True):
                save_list(j * 2 + PARTS - 1, [(i, h) for i in range(2) for h in range(2)])
                if sums:
                    relu(j - 2, 0, j - 2)
                save_list(j * 2 + PARTS)
                if sums:
                    relu(TILES + 1 - j, 1, j - 2)
                first_ids(pa)
                other_ids(1 - pa)

            step(1, 1, False)
            with act.Fori(1, PAIRS // 2) as v:
                for pa in range(2):
                    step(v * 2 + pa, pa)
            relus(PAIRS - 2)
            first[0].set(end.value(FLAT - 4 * GR))
            other_ids(1)
            relus(PAIRS - 1)
            for part in range(2):
                act.dma_start(lists[part][:, bass.ds(end.value(FLAT - 4 * GR), 2 * GR)], zids[0:HP, :]
                              ).then_inc(ends_saved, 16)

            def save_blocks(a, table, src, done, saved, ahead):
                act.wait_ge(done, a + 1)
                for t in (a * LNB, TILES - LNB - a * LNB):
                    if isinstance(t, int):
                        part = src[:, t:t + LNB, :]
                    else:
                        part = src[:, bass.ds(t, LNB), :]
                    act.dma_start(rows(table, t, ahead, LNB).rearrange("(t p) w -> p t w", p=P), part
                                  ).then_inc(saved, 16)

            for a in range(PAIRS // LNB):
                save_blocks(a, tab1, row1, block1_done, tab1_saved, 1)

            sets = Count(act, "act_sets")
            act.nop().then_inc(score_used, 1)
            end.set(0)

            def exponentials(n, score_set):
                act.drain()
                act.wait_ge(score_ready, score_set.value())
                act.activation(expo[:, 0:n], score[:, 0:n], ACT.Exp, bias=shift[:, 0:1]).then_inc(score_used, 1)

            def attend(bank, j, entry):
                part0 = isinstance(j, int) and j == 0 and bank == 0
                sets.add()
                exponentials(1, sets)
                act.drain()
                if not (isinstance(j, int) and j == 0):
                    act.wait_ge(sum_done, j * 2 + bank - 1)
                act.activation(own_diag[:, bank, :], ident[:], ACT.Copy, scale=expo[:, 0:1]).then_inc(own_ready, 1)
                for e in (range(PARTS) if part0 else [entry]):
                    until = end_of(act, e)
                    spread = to_row[:, e, :] if part0 else ident[:]
                    with act.Fori(end.value(FLAT - 4 * GR), until, 2) as s:
                        sets.add()
                        last0.set(s // 2 + 1)
                        last1.set(s // 2 + CREDIT)
                        exponentials(2, sets)
                        act.drain()
                        act.wait_ge(diag_used, last0.value())
                        act.activation(diag[:, 0, :], spread, ACT.Copy, scale=expo[:, 0:1]).then_inc(diag_ready, 1)
                        act.wait_ge(used[ATTEND], last1.value())
                        act.activation(diag[:, 1, :], spread, ACT.Copy, scale=expo[:, 1:2]).then_inc(diag_ready, 1)
                    end.set(until)

            last0, last1 = Count(act, "act_last0"), Count(act, "act_last1")
            act.wait_ge(params, 2)
            attend(0, 0, None)
            attend(1, 0, PARTS)
            with act.Fori(1, LNB) as j:
                attend(0, j, j * 2 + PARTS - 1)
                attend(1, j, j * 2 + PARTS)
            with act.Fori(1, PAIRS // LNB) as a:
                save_blocks(a - 1, out, rows_sb, block2_done, out_saved, 0)
                with act.Fori(a * LNB, a * LNB + LNB) as j:
                    attend(0, j, j * 2 + PARTS - 1)
                    attend(1, j, j * 2 + PARTS)
            save_blocks(PAIRS // LNB - 1, out, rows_sb, block2_done, out_saved, 0)

        @block.vector
        def _(dve):
            dve.memset(cnt[:], 0.0)
            dve.memset(cnt_m[:], 0.0)
            dve.memset(ofs[0:1, 0:1], 0)
            for _ in range(CREDIT):
                dve.nop().then_inc(used[MAXIMA], 1)
            dve.wait_ge(loaded, 48)
            dve.tensor_scalar(den[:, 0:1], beta_sb[:], -1.0, None, ALU.mult)
            dve.drain()
            dve.tensor_tensor(shift[:], beta_sb[:], den[:, 0:1], ALU.min).then_inc(params, 1)
            dve.wait_ge(consts, CONSTS)
            for p, n in enumerate((*LANES, 1)):
                dve.tensor_scalar(lane[:, p:p + 1], lane[:, p:p + 1], n - 1, None, ALU.bitwise_and)
                dve.drain()
                dve.tensor_scalar(first_col[:, p:p + 1], lane[:, p:p + 1], float(SLICE // n), None, ALU.mult)
                dve.drain()
            dve.nop().then_inc(params, 1)

            flat = cand[:].rearrange("p c s -> p (c s)")

            def take_columns(codes, h, remove):
                eight = slice(8 * h, 8 * h + 8)
                dve.max(top[:, eight], codes)
                dve.drain()
                dve.max_index(col[:, eight], top[:, eight], codes)
                dve.drain()
                if remove:
                    drop_columns(codes, h)

            def drop_columns(codes, h):
                dve.match_replace(codes, top[:, 8 * h:8 * h + 8], codes, 0.0)
                dve.drain()

            def expand(part):
                dve.tensor_copy(topi[:], top[:])
                dve.tensor_scalar(colf[:], col[:], first_col[:, part:part + 1], None, ALU.add)
                dve.drain()
                dve.tensor_tensor(cand[:], colf[:].rearrange("p (c a) -> p c a", a=1).to_broadcast([P, COLS, SLICES]),
                                  base[:].rearrange("p (a s) -> p a s", a=1).to_broadcast([P, COLS, SLICES]), ALU.add)
                dve.tensor_tensor(bits[:], topi[:].rearrange("p (c a) -> p c a", a=1).to_broadcast([P, COLS, SLICES]),
                                  bit[:].rearrange("p (a s) -> p a s", a=1).to_broadcast([P, COLS, SLICES]),
                                  ALU.bitwise_and)
                dve.drain()
                dve.scalar_tensor_tensor(cand[:], bits[:], 0.0, cand[:], ALU.is_gt, ALU.mult)
                dve.drain()
                dve.tensor_scalar(is_set[:, 0:COLS * SLICES], flat, 0.0, 0.0, ALU.is_gt, ALU.add,
                                  accum_out=cnt[:, 1:2])
                dve.drain()

            def most_of_rows():
                dve.transpose(cnt_t[:], cnt[:])
                dve.drain()
                dve.tensor_reduce(cnt_m[:, 0:1], cnt_t[:], AX.X, ALU.max)
                dve.drain()
                dve.transpose(cnt_u[:], cnt_m[:])
                dve.drain()
                for b in range(4):
                    dve.tensor_copy(cnt_q[0:1, b, :], cnt_u[32 * b:32 * b + 1, 0:2])
                dve.drain()
                dve.tensor_reduce(most[0:1, :], cnt_q[0:1].rearrange("p b c -> p c b"), AX.X, ALU.max)
                dve.drain()
                dve.tensor_copy(mosti[0:1, :], most[0:1, :])
                dve.drain()

            def emit(slot):
                dve.max(best[:], flat)
                dve.drain()
                dve.tensor_copy(list_sb[:, slot:slot + 8] if isinstance(slot, int)
                                else list_sb[:, bass.ds(slot, 8)], best[:])
                dve.match_replace(flat, best[:], flat, 0.0)
                dve.drain()

            slot = Count(dve, "dve_slot")

            def emit_more():
                emit(slot.value(N - 8))
                slot.add(8)
                dve.tensor_scalar(length[:], length[:], 8.0, None, ALU.add)
                dve.drain()

            def zeros_behind():
                dve.tensor_copy(list_sb[:, bass.ds(slot.value(N), 2 * GR)], zids[:])

            def extract(entry, part, codes, after=None):
                dve.tensor_scalar(is_set[:, 0:codes.shape[1]], codes, 0.0, 0.0, ALU.is_gt, ALU.add,
                                  accum_out=cnt[:, 0:1])
                take_columns(codes, 0, True)
                take_columns(codes, 1, False)
                expand(part)
                most_of_rows()
                dve.wait_ge(list_saved, entry + 1)
                dve.tensor_scalar(lengthi[:], most[0:1, 1:2], 1.0, 1.0, ALU.max, ALU.add)
                dve.memset(list_sb[:, COLS:COLS + 2 * GR], 0)
                dve.drain()
                dve.tensor_scalar(lengthi[:], lengthi[:], 1, 1, ALU.logical_shift_right, ALU.logical_shift_left)
                emit(0)
                dve.tensor_copy(length[:], lengthi[:])
                emit(8)
                columns = dve.value_load(mosti[0:1, 0:1], min_val=0, max_val=N)
                entries = dve.value_load(mosti[0:1, 1:2], min_val=0, max_val=N)
                slot.set(COLS)
                with dve.If(entries > COLS):
                    dve.memset(length[:], float(COLS))
                    dve.drain()
                    with dve.Fori(COLS, entries, 8):
                        emit_more()
                    zeros_behind()
                    dve.drain()
                with dve.If(columns > COLS):
                    with dve.If(entries <= COLS):
                        dve.memset(length[:], float(COLS))
                        dve.drain()
                    drop_columns(codes, 1)
                    with dve.Fori(COLS, columns, COLS):
                        take_columns(codes, 0, True)
                        take_columns(codes, 1, True)
                        expand(part)
                        most_of_rows()
                        ids = dve.value_load(mosti[0:1, 1:2], min_val=0, max_val=N)
                        with dve.Fori(0, ids, 8):
                            emit_more()
                        dve.nop()
                    zeros_behind()
                    dve.drain()
                this, next_ = ((ofs[0:1, entry:entry + 1], ofs[0:1, entry + 1:entry + 2]) if isinstance(entry, int)
                               else (ofs[0:1, bass.ds(entry, 1)], ofs[0:1, bass.ds(entry + 1, 1)]))
                dve.drain()
                dve.tensor_tensor(next_, this, length[:], ALU.add)
                if after is not None:
                    dve.drain().then_inc(after, 1)
                    dve.nop().then_inc(list_ready, 1)
                else:
                    dve.drain().then_inc(list_ready, 1)

            dve.wait_ge(part_in, 16 * PARTS)
            for p in range(PARTS):
                extract(p, p, part_code[p][:])
            dve.wait_ge(code_ready[1], 1)
            extract(PARTS, PARTS, code[1][:], code_used[1])
            with dve.Fori(1, PAIRS) as j:
                for bank in range(2):
                    dve.wait_ge(code_ready[bank], j + 1)
                    extract(j * 2 + PARTS - 1 + bank, PARTS, code[bank][:], code_used[bank])

            def rsqrt(y, v, a, b):
                dve.tensor_scalar(a.bitcast(i32), v.bitcast(i32), 1, None, ALU.logical_shift_right)
                dve.drain()
                dve.tensor_scalar(y.bitcast(i32), a.bitcast(i32), -1.0, float(0x5F3759DF), ALU.mult, ALU.add)
                dve.drain()
                for _ in range(4):
                    dve.tensor_tensor(a, y, y, ALU.mult)
                    dve.drain()
                    dve.scalar_tensor_tensor(b, a, -0.5, v, ALU.mult, ALU.mult)
                    dve.drain()
                    dve.scalar_tensor_tensor(y, b, 1.5, y, ALU.add, ALU.mult)
                    dve.drain()

            T = 2 * LNB

            def tile_of(a, k):
                return (a * LNB + k) if k < LNB else (TILES - LNB - a * LNB + k - LNB)

            def normalise(buf, a):
                dve.drain()
                for k in range(T):
                    dve.bn_stats(stats[:, k, :], at(buf, tile_of(a, k))[:, 0:F])
                dve.drain()
                for k in range(T):
                    dve.bn_aggr(mv[:, k, :], stats[:, k, :])
                dve.drain()
                dve.tensor_scalar(nw[:, 0, :], mv[:, :, 1], LN_EPS, None, ALU.add)
                dve.drain()
                rsqrt(nw[:, 1, :], nw[:, 0, :], nw[:, 2, :], nw[:, 3, :])
                for k in range(T):
                    row = at(buf, tile_of(a, k))[:, 0:F]
                    dve.tensor_scalar(row, row, mv[:, k, 0:1], nw[:, 1, k:k + 1], ALU.subtract, ALU.mult)
                dve.drain()

            end = Count(dve, "dve_end")

            def maximum(entry):
                dve.memset(most2[:], 0.0)
                dve.drain()
                until = end_of(dve, entry)
                with dve.Fori(end.value(FLAT - 4 * GR), until, 2) as s:
                    dve.wait_ge(landed[MAXIMA], s // QD + 2)
                    dve.tensor_tensor(most2[:], most2[:], got[:, bass.ds(s % RINGS, 2), 0:F], ALU.max
                                      ).then_inc(used[MAXIMA], 1)
                    dve.drain()
                end.set(until)
                dve.tensor_tensor(pooled[:], most2[:, 0, :], most2[:, 1, :], ALU.max)

            def add_maximum(t, of=pooled):
                dve.drain()
                dve.tensor_tensor(pooled[:], of[:] if of is pooled else of, at(rows_sb, t), ALU.max)
                dve.drain()
                row = at(row1, t)[:, 0:F]
                dve.tensor_tensor(row, row, pooled[:], ALU.add)

            for p, (n, r) in enumerate(zip(LANES, PART_ROW)):
                maximum(p)
                dve.drain().then_inc(part_done, 1)
                dve.wait_ge(part_turned, p + 1)
                dve.tensor_reduce(pooledT[:, r:r + P // n], ps_t[:, 0, :].rearrange("f (r l) -> f r l", l=n),
                                  AX.X, ALU.max)
                dve.drain()
            dve.nop().then_inc(pooledT_ready, 1)
            dve.wait_ge(pooledT_turned, 1)
            dve.wait_ge(x_again, 64)
            for i in range(2):
                dve.wait_ge(relu_done[i], PAIRS)
            dve.wait_ge(list_saved, ENTRIES + 1)
            add_maximum(0, ps_t[:, 1, :])
            maximum(PARTS)
            add_maximum(TILES - 1)

            def pair_of_maxima(j):
                maximum(j * 2 + PARTS - 1)
                add_maximum(j)
                maximum(j * 2 + PARTS)
                add_maximum(TILES - 1 - j)

            def finish_layer0(a):
                normalise(row1, a)
                for k in range(T):
                    row = at(row1, tile_of(a, k))[:, 0:F]
                    dve.scalar_tensor_tensor(squares[:, k, :], row, 1.0, row, ALU.mult, ALU.mult,
                                             accum_out=nw[:, 4, k:k + 1])
                dve.drain()
                rsqrt(nw[:, 1, :], nw[:, 4, :], nw[:, 2, :], nw[:, 3, :])
                for half in range(2):
                    t = tile_of(a, half * LNB)
                    some = row1[:, t:t + LNB, :] if isinstance(t, int) else row1[:, bass.ds(t, LNB), :]
                    k = slice(half * LNB, half * LNB + LNB)
                    dve.tensor_tensor(some[:, :, F], nw[:, 4, k], nw[:, 1, k], ALU.mult)
                    dve.memset(some[:, :, F + 1:TW], 1.0) if isinstance(t, int) else \
                        dve.tensor_scalar(some[:, :, F + 1:TW], some[:, :, 0:TW - F - 1], 0.0, 1.0, ALU.mult, ALU.add)
                dve.drain().then_inc(block1_done, 1)

            with dve.Fori(1, LNB) as j:
                pair_of_maxima(j)
            finish_layer0(0)
            with dve.Fori(1, PAIRS // LNB) as a:
                with dve.Fori(0, LNB) as k:
                    pair_of_maxima(a * LNB + k)
                finish_layer0(a)

            end.set(0)
            sets = Count(dve, "dve_sets")
            dve.wait_ge(ownl_done, 1)
            for p in range(PARTS):
                dve.tensor_copy(ownl[:, p, 0:F], ps_h[:, p, :])
                dve.tensor_copy(ownl[:, p, F:TW], ps_t[:, p, 0:TW - F])
            dve.drain()

            def give_scores(n, dots, norms, norm):
                dve.tensor_scalar(den[:, 0:n], norms, norm, COS_EPS, ALU.mult, ALU.add)
                dve.drain()
                dve.reciprocal(den[:, 0:n], den[:, 0:n])
                sets.add()
                dve.drain()
                dve.wait_ge(score_used, sets.value())
                dve.scalar_tensor_tensor(score[:, 0:n], dots, beta_sb[:, 0:1], den[:, 0:n], ALU.mult, ALU.mult
                                         ).then_inc(score_ready, 1)

            def own_scores(t, bank):
                dve.drain()
                dve.tensor_copy(ownc[bank][:], at(row1, t))
                dve.drain()
                norm = ownc[bank][:, F:F + 1]
                dve.tensor_tensor(dots[:, 0:1], norm, norm, ALU.mult)
                dve.drain()
                give_scores(1, dots[:, 0:1], norm, norm)

            place, quad = Count(dve, "dve_place"), Count(dve, "dve_quad")

            def scores(entry, own):
                until = end_of(dve, entry)
                with dve.Fori(end.value(FLAT - 4 * GR), until, 2) as s:
                    place.set(s % RINGS)
                    quad.set(s // QD + 2)
                    dve.drain()
                    dve.wait_ge(landed[ATTEND], quad.value())
                    pair = got[:, bass.ds(place.value(RINGS - 2), 2), :]
                    for i in range(2):
                        dve.scalar_tensor_tensor(prod[:, i, :], pair[:, i, 0:F], 1.0, own[:, 0:F], ALU.mult, ALU.mult,
                                                 accum_out=dots[:, i:i + 1])
                    give_scores(2, dots[:], pair[:, :, F], own[:, F:F + 1])
                end.set(until)

            def finish(t, bank, n):
                dve.wait_ge(sum_done, n + 1)
                dve.reciprocal(nw[:, 5, bank:bank + 1], wsum[bank][:, F + 1:F + 2])
                dve.drain()
                row = at(rows_sb, t)
                dve.scalar_tensor_tensor(row, wsum[bank][:, 0:F], nw[:, 5, bank:bank + 1], ownc[bank][:, 0:F],
                                         ALU.mult, ALU.add).then_inc(sum_used, 1)

            own_scores(0, 0)
            for p in range(PARTS):
                scores(p, ownl[:, p, :])
            own_scores(TILES - 1, 1)
            scores(PARTS, ownc[1])
            finish(0, 0, 0)

            def pair_of_tiles(j, first=False):
                own_scores(j, 0)
                scores(j * 2 + PARTS - 1, ownc[0])
                if not first:
                    finish(TILES - j, 1, j * 2 - 1)
                own_scores(TILES - 1 - j, 1)
                scores(j * 2 + PARTS, ownc[1])
                finish(j, 0, j * 2)

            def finish_layer1(a):
                j = a * LNB + LNB - 1
                finish(TILES - 1 - j, 1, j * 2 + 1)
                normalise(rows_sb, a)
                dve.nop().then_inc(block2_done, 1)

            with dve.Fori(1, LNB) as j:
                pair_of_tiles(j)
            finish_layer1(0)
            with dve.Fori(1, PAIRS // LNB) as a:
                pair_of_tiles(a * LNB, True)
                with dve.Fori(1, LNB) as k:
                    pair_of_tiles(a * LNB + k)
                finish_layer1(a)


_INS = ["x", "adj", "L0_gnn_weight", "L0_gnn_bias", "L1_gnn_beta"]


def kernel(**inputs):
    import concourse.bacc as bacc
    from concourse.bass_utils import run_bass_kernel_spmd as run

    nc = bacc.Bacc("TRN2", target_bir_lowering=False, num_devices=1)
    arrays = {n: np.ascontiguousarray(inputs[n]) for n in _INS}
    args = [nc.dram_tensor(f"in_{n}", a.shape, mybir.dt.from_np(a.dtype), kind="ExternalInput").ap()
            for n, a in arrays.items()]
    out = nc.dram_tensor("out", inputs["x"].shape, mybir.dt.float32, kind="ExternalOutput").ap()
    adj_resnorm_program(nc, *args, out)
    r = run(nc, [{f"in_{n}": a for n, a in arrays.items()}], core_ids=[0])
    return r.results[0]["out"]
```

```python
import numpy as np
import concourse.bass as bass
from concourse import mybir
from contextlib import ExitStack


def adj_resnorm_program(nc, x, adj, weight, bias, beta, out):
    fp32, bf16 = mybir.dt.float32, mybir.dt.bfloat16
    u32, i32 = mybir.dt.uint32, mybir.dt.int32
    ALU = mybir.AluOpType
    ACT = mybir.ActivationFunctionType
    AX = mybir.AxisListType

    P = 128
    N, F = adj.shape[0], weight.shape[1]
    TILES = N // P
    SLICE = 512
    SLICES = N // SLICE
    PER = SLICE // P
    SUBS = 4
    SUBW = N // SUBS
    SPS = SUBW // SLICE
    LANES = (8, 8, 4, 2)
    PART_ROW = (0, 16, 32, 64)
    PARTS = len(LANES)
    ENTRIES = PARTS + TILES - 1
    PAIRS = TILES // 2
    COLS = 16
    GR = 16
    QD = 4
    RINGS = 32
    CREDIT = RINGS // 2
    LAG = 3
    SHORTEST = (LAG + 1) * QD // 2
    QUAD, IDS = 16 * QD, 32
    TW = F + 4
    FLAT = ENTRIES * N + 4 * GR
    HC = 4
    CHUNKS = TILES // HC
    LNB = 8
    LN_EPS, COS_EPS = 1e-5, 1e-7

    HP = P // 2
    lists = [nc.dram_tensor(f"lists{i}", [HP, FLAT], u32, kind="Internal").ap() for i in range(2)]
    codes0 = nc.dram_tensor("codes0", [P, SLICE], fp32, kind="Internal").ap()
    tab_h = nc.dram_tensor("tab_h", [N + 1, F], fp32, kind="Internal").ap()
    tab0 = nc.dram_tensor("tab0", [N + 1, F], fp32, kind="Internal").ap()
    tab1 = nc.dram_tensor("tab1", [N + 1, TW], fp32, kind="Internal").ap()

    ctx = ExitStack()
    with ctx:
        def sb(name, shape, dt):
            return ctx.enter_context(nc.sbuf_tensor(name, shape, dt))

        def pb(name, shape, dt):
            return ctx.enter_context(nc.psum_tensor(name, shape, dt))

        def sem(name):
            return ctx.enter_context(nc.semaphore(name))

        big = sb("big", [P, 2 * SUBS * SUBW], fp32)
        row1 = big[:, 0:TILES * TW].rearrange("p (t w) -> p t w", w=TW)
        rows_sb = sb("rows_sb", [P, TILES, F], fp32)
        list_sb = sb("list_sb", [P, N + 3 * GR], u32)
        head = [sb(f"head{i}", [P, 2 * GR], u32) for i in range(2)]
        ofs = sb("ofs", [1, ENTRIES + 1], u32)
        got = sb("got", [P, 2 * RINGS + 1, TW], fp32)
        idx = [[sb(f"idx{i}_{h}", [P, GR], u32) for h in range(2)] for i in range(2)]
        stage = got[:].rearrange("p k w -> p (k w)")[:, 0:4 * HC * P].rearrange("p (b t f) -> p b t f", b=4, t=HC)
        squares = list_sb[:, 0:2 * LNB * F].bitcast(fp32).rearrange("p (k f) -> p k f", f=F)
        xs = [stage[:, i] for i in range(2)]        
        xT = [stage[:, 2 + i] for i in range(2)]
        pow_id = sb("pow_id", [P, SLICES, P], bf16)
        neg_id = sb("neg_id", [P, P], bf16)
        ident = sb("ident", [P, P], fp32)
        to_row = sb("to_row", [P, PARTS, P], fp32)
        to_lane = sb("to_lane", [P, PARTS, P], fp32)
        bit = sb("bit", [P, SLICES], i32)
        base = sb("base", [P, SLICES], fp32)
        lane = sb("lane", [P, PARTS + 1], i32)
        first_col = sb("first_col", [P, PARTS + 1], fp32)
        code0 = sb("first_code", [P, SLICE], fp32)
        part_code = [sb(f"part_code{i}", [P, SLICE // LANES[i]], fp32) for i in range(PARTS)]
        is_set = sb("is_set", [P, SLICE], bf16)
        top = sb("top", [P, COLS], fp32)
        topi = sb("topi", [P, COLS], i32)
        col = sb("col", [P, COLS], u32)
        colf = sb("colf", [P, COLS], fp32)
        bits = sb("bits", [P, COLS, SLICES], i32)
        cand = sb("cand", [P, COLS, SLICES], fp32)
        best = sb("best", [P, 8], fp32)
        cnt = sb("cnt", [P, 32], fp32)
        cnt_t = sb("cnt_t", [P, 32], fp32)
        cnt_m = sb("cnt_m", [P, 32], fp32)
        cnt_u = sb("cnt_u", [P, 32], fp32)
        cnt_q = sb("cnt_q", [1, 4, 2], fp32)
        most = sb("most", [1, 2], fp32)
        mosti = sb("mosti", [1, 3], u32)
        length = sb("length", [1, 1], fp32)
        lengthi = sb("lengthi", [1, 1], i32)
        w_sb = sb("w_sb", [P, F], fp32)
        bias_sb = sb("bias_sb", [1, F], fp32)
        ones = sb("ones", [1, P], fp32)
        beta_sb = sb("beta_sb", [P, 1], fp32)
        shift = sb("shift", [P, 1], fp32)
        zeros = sb("zeros", [P, TW], fp32)
        zids = sb("zids", [P, 2 * GR], u32)
        most2 = sb("most2", [P, 2, F], fp32)
        pooled = sb("pooled", [P, F], fp32)
        pooledT = sb("pooledT", [P, P], fp32)
        ownc = [sb(f"ownc{i}", [P, TW], fp32) for i in range(2)]
        ownl = sb("ownl", [P, PARTS, TW], fp32)
        prod = sb("prod", [P, 4, F], fp32)
        dots = sb("dots", [P, 4], fp32)
        den = sb("den", [P, 4], fp32)
        score = sb("score", [P, 4], fp32)
        expo = sb("expo", [P, 4], fp32)
        diag = sb("diag", [P, 2, P], fp32)
        own_score = sb("own_score", [P, TILES], fp32)
        own_den = sb("own_den", [P, TILES], fp32)
        own_expo = sb("own_expo", [P, TILES], fp32)
        own_diag = sb("own_diag", [P, 2, P], fp32)
        stats = sb("stats", [P, 2 * LNB, 6], fp32)
        mv = sb("mv", [P, 2 * LNB, 2], fp32)
        nw = sb("nw", [P, 6, 2 * LNB], fp32)

        code = [pb(f"code_ps{i}", [P, SLICE], fp32) for i in range(2)]
        ps_t = pb("ps_t", [P, HC, P], fp32)
        ps_h = pb("ps_h", [P, HC, F], fp32)
        agg = [pb(f"agg{i}", [P, F], fp32) for i in range(2)]
        wsum = [pb(f"wsum{i}", [P, TW], fp32) for i in range(2)]

        consts = sem("consts")
        params = sem("params")
        loaded = sem("loaded")
        x_in = [sem(f"x_in{i}") for i in range(2)]
        x_turned = sem("x_turned")
        xT_copied = sem("xT_copied")
        h_done = sem("h_done")
        h_copied = sem("h_copied")
        h_saved = sem("h_saved")
        adj_in = [sem(f"adj_in{i}") for i in range(2 * SUBS)]
        adj_used = sem("adj_used")
        code_ready = [sem(f"code_ready{i}") for i in range(2)]
        code_used = [sem(f"code_used{i}") for i in range(2)]
        code0_saved = sem("code0_saved")
        part_in = sem("part_in")
        list_ready = sem("list_ready")
        list_saving = sem("list_saving")
        list_saved = sem("list_saved")
        ends_saved = sem("ends_saved")
        SUMS, MAXIMA, ATTEND = range(3)
        idx_in = [[[sem(f"idx_in{w}_{i}_{h}") for h in range(2)] for i in range(2)] for w in range(3)]
        quad_in = [[[sem(f"quad_in{w}_{r}_{i}") for i in range(LAG + 1)] for r in range(2)] for w in range(3)]
        landed = [sem(f"landed{w}") for w in range(3)]
        used = [sem(f"used{w}") for w in range(3)]
        agg_done = [sem(f"agg_done{i}") for i in range(2)]
        relu_done = [sem(f"relu_done{i}") for i in range(2)]
        tab0_saved = sem("tab0_saved")
        x_again = sem("x_again")
        part_done = sem("part_done")
        part_turned = sem("part_turned")
        pooledT_ready = sem("pooledT_ready")
        pooledT_turned = sem("pooledT_turned")
        block1_done = sem("block1_done")
        tab1_saved = sem("tab1_saved")
        ownl_done = sem("ownl_done")
        own_scored = sem("own_scored")
        own_copied = sem("own_copied")
        own_ready = sem("own_ready")
        score_ready = sem("score_ready")
        score_used = sem("score_used")
        diag_ready = sem("diag_ready")
        diag_used = sem("diag_used")
        sum_done = sem("sum_done")
        sum_used = sem("sum_used")
        block2_done = sem("block2_done")
        out_saved = sem("out_saved")
        zeros_saved = sem("zeros_saved")

        block = ctx.enter_context(nc.Block())
        CONSTS = 8 + 2 + 3 * SLICES + 4 * PARTS + PARTS + 1

        class Count:

            def __init__(self, e, name):
                self.e, self.r = e, e.alloc_register(name)
                e.reg_mov(self.r, 0)

            def value(self, most=1 << 22):
                return self.e.snap(self.r, min_val=0, max_val=most)

            def set(self, v):
                self.e.reg_mov(self.r, v)

            def add(self, n=1):
                self.e.reg_add(self.r, self.r, n)

        def within(v, least, most, why="slots lie within the lists at their longest"):
            return nc.s_assert_within(v, least, most, skip_runtime_bounds_check_because=why)

        def end_of(e, entry):
            return e.value_load(ofs[0:1, entry + 1:entry + 2] if isinstance(entry, int)
                                else ofs[0:1, bass.ds(entry + 1, 1)], min_val=2, max_val=FLAT - 4 * GR)

        def at(buf, t):
            return buf[:, t, :] if isinstance(t, int) else buf[:, bass.ds(t, 1), :].rearrange("p a f -> p (a f)")

        def rows(table, t, ahead, tiles=1):
            if isinstance(t, int):
                return table[t * P + ahead:(t + tiles) * P + ahead, :]
            return table[bass.ds(t * P + ahead, tiles * P), :]

        def by_four(e, slot, until, do):
            whole = (until - slot.value(FLAT)) // 4 * 4
            with e.Fori(0, whole, 4):
                do(slot.value(FLAT), 2)
                slot.add(4)
            with e.If(until > slot.value(FLAT)):
                do(slot.value(FLAT), 1)
            e.nop()
            slot.set(until)

        ids_at = {}

        def load_ids(e, which, pa, start, n, first=True, others=True, told=None):
            ahead, from_ = ids_at[e]

            def half(q, h, wait=None):
                ahead.set(start + q + h * GR)
                if wait is not None:
                    e.wait_ge(*wait)
                from_.set(ahead.value())
                begin = from_.value(FLAT - 2 * GR)
                for part in range(2):
                    e.dma_start(idx[pa][h][part * HP:(part + 1) * HP, :],
                                lists[part][:, bass.ds(begin, GR)]).then_inc(idx_in[which][pa][h], 16)
                if told:
                    told[pa][h].add()

            def free(r, h):
                if which == SUMS:
                    return used[which], (start + r + QD) // 2 + h * (GR // 2) + CREDIT - GR // 2
                return landed[which], r // QD + h * (GR // QD)

            if first:
                half(0, 0)
                with e.If(n > GR):
                    half(0, 1)
                e.nop()
            if others:
                with e.If(n > 2 * GR):
                    with e.Fori(2 * GR - QD, n - QD, 2 * GR) as r:
                        half(r + QD, 0, free(r, 0))
                        with e.If(n > r + QD + GR):
                            half(r + QD, 1, free(r, 1))
                        e.nop()
                    e.nop()
                e.nop()

        @block.sync
        def _(sp):
            sp.dma_start(w_sb[:], weight).then_inc(loaded, 16)
            sp.dma_start(bias_sb[:], bias.rearrange("(a f) -> a f", a=1)).then_inc(loaded, 16)
            sp.dma_start(beta_sb[:], beta.rearrange("(a f) -> a f", a=1).to_broadcast([P, 1])).then_inc(loaded, 16)

            def load_tile(t, bank, j):
                for s in range(SUBS):
                    i = bank * SUBS + s
                    if not isinstance(j, int):
                        sp.wait_ge(adj_used, (j - 1) * 2 * SUBS + i + 1)
                    sp.dma_start(big[:, i * SUBW:(i + 1) * SUBW],
                                 rows(adj, t, 0)[:, s * SUBW:(s + 1) * SUBW]).then_inc(adj_in[i], 16)

            load_tile(0, 0, 0)
            load_tile(TILES - 1, 1, 0)
            back = Count(sp, "sp_back")
            back.set(TILES - 1)
            with sp.Fori(1, PAIRS) as j:
                load_tile(j, 0, j)
                back.add(-1)
                load_tile(back.value(TILES - 1), 1, j)

            ids_at[sp] = (Count(sp, "sp_ahead"), Count(sp, "sp_from"))
            sp.wait_ge(adj_used, TILES * SUBS)
            n = TILES // 4
            for c in range(4):
                sp.dma_start(row1[:, c * n:(c + 1) * n, 0:F], x[c * n * P:(c + 1) * n * P, :]
                             .rearrange("(t p) f -> p t f", p=P)).then_inc(x_again, 16)
            sp.wait_ge(list_ready, ENTRIES)
            total = end_of(sp, ENTRIES - 1)
            sp.wait_ge(ends_saved, 32)
            for i in range(2):
                sp.wait_ge(agg_done[i], PAIRS)
            load_ids(sp, MAXIMA, 0, 0, total)
            sp.wait_ge(block1_done, PAIRS // LNB)
            load_ids(sp, ATTEND, 0, 0, total)
            sp.wait_ge(out_saved, 2 * 16 * PAIRS // LNB)

        @block.gpsimd
        def _(pool):
            for m in (ident, pow_id, neg_id, zeros, zids):
                pool.memset(m[:], 0.0 if m is not zids else 0).then_inc(consts, 1)
            for m in (ones, to_row, to_lane):
                pool.memset(m[:], 1.0).then_inc(consts, 1)
            pool.wait_ge(consts, 8)
            for m, fill in ((ident, 1.0), (neg_id, -1.0)):
                pool.affine_select(out=m[:], in_=m[:], compare_op=ALU.not_equal, fill=fill, base=0,
                                   pattern=[[-1, P]], channel_multiplier=1).then_inc(consts, 1)
            for s in range(SLICES):
                pool.affine_select(out=pow_id[:, s, :], in_=pow_id[:, s, :], compare_op=ALU.not_equal,
                                   fill=float(1 << s), base=0, pattern=[[-1, P]],
                                   channel_multiplier=1).then_inc(consts, 1)
                pool.memset(bit[:, s:s + 1], 1 << s).then_inc(consts, 1)
                pool.memset(base[:, s:s + 1], float(s * SLICE + 1)).then_inc(consts, 1)
            for p in range(PARTS + 1):
                pool.iota(lane[:, p:p + 1], pattern=[[0, 1]], base=0, channel_multiplier=1).then_inc(consts, 1)
            for sign in (1, -1):
                for p, (n, r) in enumerate(zip(LANES, PART_ROW)):
                    b = n * r if sign > 0 else n - 1 - n * r
                    pool.affine_select(out=to_row[:, p, :], in_=to_row[:, p, :], compare_op=ALU.is_ge, fill=0.0,
                                       base=b, pattern=[[-sign * n, P]], channel_multiplier=sign).then_inc(consts, 1)
                    pool.affine_select(out=to_lane[:, p, :], in_=to_lane[:, p, :], compare_op=ALU.is_ge, fill=0.0,
                                       base=b, pattern=[[sign, P]], channel_multiplier=-sign * n).then_inc(consts, 1)
                if sign > 0:
                    pool.wait_ge(consts, CONSTS - 2 * PARTS)

            issued = [[Count(pool, f"issued{r}_{i}") for i in range(LAG + 1)] for r in range(2)]
            taken = [[Count(pool, f"taken{i}_{h}") for h in range(2)] for i in range(2)]

            def start_counts(which):
                for r in range(2):
                    for i in range(2):
                        pool.nop().then_inc(idx_in[which][r][i], IDS)
                        taken[r][i].set(1)
                    for i in range(LAG + 1):
                        issued[r][i].set(0)

            def have_landed(which, r, i):
                pool.wait_ge(quad_in[which][r][i], issued[r][i].value() * QUAD)

            def landed_so_far(which, pa, i, starts, very_first):
                if starts and i < LAG - 1:
                    return
                if starts and i == LAG - 1:
                    if not very_first:
                        for k in range(LAG + 1):
                            have_landed(which, 1 - pa, k)
                    pool.nop().then_inc(landed[which], LAG)
                else:
                    have_landed(which, pa, (i + 1) % (LAG + 1))
                    pool.nop().then_inc(landed[which], 1)

            def gather(which, pa, table, width, start, n, q, first, whole, very_first=False):
                def quad(i):
                    h, k0 = i // 4, i % 4 * QD
                    if i % 4 == 0:
                        taken[pa][h].add()
                        pool.wait_ge(idx_in[which][pa][h], taken[pa][h].value() * IDS)
                    if not first or i >= RINGS // QD:
                        pool.wait_ge(used[which], (start + q) // 2 + 2 * i + 2)
                    issued[pa][i % (LAG + 1)].add()
                    for k in range(k0, k0 + QD):
                        pool.indirect_dma_start(
                            out=got[:, pa * RINGS + (i * QD + k - k0) % RINGS, 0:width], out_offset=None, in_=table,
                            in_offset=bass.IndirectOffsetOnAxis(ap=idx[pa][h][:, k:k + 1], axis=0),
                        ).then_inc(quad_in[which][pa][i % (LAG + 1)], 16)
                    landed_so_far(which, pa, i, first, very_first)
                    if i + 1 < 8:
                        if whole:
                            quad(i + 1)
                        else:
                            with pool.If(n > q + QD * (i + 1)):
                                quad(i + 1)
                            pool.nop()

                quad(0)

            def all_landed(which, rings):
                for r in range(rings):
                    for i in range(LAG + 1):
                        have_landed(which, r, i)
                pool.nop().then_inc(landed[which], LAG)

            start_counts(SUMS)
            start, before = Count(pool, "pool_start"), Count(pool, "pool_before")
            pool.wait_ge(h_saved, 16 * CHUNKS)
            pool.wait_ge(zeros_saved, 16 * 3)

            def sums(last_entry, entries, pa, very_first=False):
                pool.wait_ge(list_ready, entries)
                end = end_of(pool, last_entry)
                s = start.value(FLAT - 4 * GR)
                n = within(end - s, 4, FLAT)
                pool.wait_ge(used[SUMS], before.value() // 2 + CREDIT)
                gather(SUMS, pa, tab_h, F, s, n, 0, True, False, very_first)
                with pool.If(n > 32):
                    with pool.Fori(32, n, 32) as q:
                        gather(SUMS, pa, tab_h, F, s, n, q, False, False)
                    pool.nop()
                pool.nop()
                before.set(s)
                start.set(end)

            sums(PARTS, PARTS + 1, 0, True)
            sums(PARTS + 2, PARTS + 3, 1)
            with pool.Fori(1, PAIRS // 2) as v:
                for pa in range(2):
                    last = v * 4 + 2 * pa + PARTS
                    sums(last, last + 1, pa)
            all_landed(SUMS, 2)

            total = end_of(pool, ENTRIES - 1)
            for which, saved, value, table, width in ((MAXIMA, tab0_saved, 16 * TILES, tab0, F),
                                                      (ATTEND, tab1_saved, 32 * PAIRS // LNB, tab1, TW)):
                start_counts(which)
                pool.wait_ge(saved, value)
                gather(which, 0, table, width, 0, total, 0, True, True, True)
                with pool.Fori(2 * GR, total - 2 * GR + 1, 2 * GR) as q:
                    gather(which, 0, table, width, 0, total, q, False, True)
                rest = within(total // (2 * GR) * (2 * GR), 2 * GR, FLAT)
                with pool.If(total > rest):
                    gather(which, 0, table, width, 0, total, rest, False, False)
                pool.nop()
                all_landed(which, 1)

        @block.tensor
        def _(pe):
            pe.wait_ge(consts, CONSTS)
            pe.wait_ge(loaded, 48)
            for w in (SUMS, ATTEND):
                for _ in range(CREDIT):
                    pe.nop().then_inc(used[w], 1)
            pe.nop().then_inc(diag_used, 1)

            def codes(bank, j, c, s):
                for sub in range(SUBS):
                    i = bank * SUBS + sub
                    pe.wait_ge(adj_in[i], j * 16 + 16)
                    high = big[:, i * SUBW:(i + 1) * SUBW].bitcast(bf16)
                    for k in range(SPS):
                        mm = pe.matmul(code[bank][:], pow_id[:, sub * SPS + k, :],
                                       high[:, 2 * SLICE * k + 1:2 * SLICE * (k + 1):2],
                                       start=(sub == 0 and k == 0), stop=(sub == SUBS - 1 and k == SPS - 1))
                    mm.then_inc(adj_used, 1)
                pe.matmul(code[bank][:, c * P:(c + 1) * P], at(pow_id, s), neg_id[:],
                          start=False, stop=True, skip_group_check=True).then_inc(code_ready[bank], 1)

            codes(0, 0, 0, 0)

            def turn(c, i):
                pe.wait_ge(x_in[i], c // 2 * 16 + 16)
                if not (isinstance(c, int) and c == 0):
                    pe.wait_ge(xT_copied, c)
                for k in range(HC):
                    mm = pe.transpose(ps_t[:, k, :], xs[i][:, k, :], ident[:])
                mm.then_inc(x_turned, 1)

            def times_w(c, i):
                pe.wait_ge(xT_copied, c + 1)
                if not (isinstance(c, int) and c == 0):
                    pe.wait_ge(h_copied, c)
                for k in range(HC):
                    mm = pe.matmul(ps_h[:, k, :], xT[i][:, k, :], w_sb[:], start=True, stop=True)
                mm.then_inc(h_done, 1)

            turn(0, 0)
            turn(1, 1)
            times_w(0, 0)
            with pe.Fori(1, CHUNKS // 2) as v:
                for i in range(2):
                    turn(v * 2 + i, i)
                    times_w(v * 2 + i - 1, 1 - i)
            times_w(CHUNKS - 1, 1)

            end, quads, slots = Count(pe, "pe_end"), Count(pe, "pe_quads"), Count(pe, "pe_slots")

            def add_neighbours(entry, pa, bank, lhsT):
                pe.wait_ge(list_ready, entry + 1)
                until = end_of(pe, entry)
                with pe.Fori(end.value(FLAT - 4 * GR), until, 2):
                    pe.wait_ge(landed[SUMS], slots.value() // QD + quads.value() + LAG + 1)
                    k = slots.value() % RINGS + pa * RINGS
                    pe.matmul(agg[bank][:], lhsT, at(got, k)[:, 0:F], start=False, stop=False, skip_group_check=True)
                    pe.matmul(agg[bank][:], lhsT, at(got, k + 1)[:, 0:F], start=False, stop=False,
                              skip_group_check=True).then_inc(used[SUMS], 1)
                    slots.add(2)
                end.set(until)

            def aggregate(t, bank, j, pa, entry):
                if not isinstance(j, int):
                    pe.wait_ge(relu_done[bank], j)
                elif j > 0:
                    pe.wait_ge(relu_done[bank], j)
                else:
                    pe.wait_ge(h_copied, CHUNKS)
                pe.matmul(agg[bank][:], ones[:], bias_sb[:], start=True, stop=False, skip_group_check=True)
                pe.matmul(agg[bank][:], ident[:], at(rows_sb, t), start=False, stop=False, skip_group_check=True)
                if isinstance(j, int) and j == 0 and bank == 0:
                    for p in range(PARTS):
                        add_neighbours(p, pa, bank, to_row[:, p, :])
                else:
                    add_neighbours(entry, pa, bank, ident[:])
                pe.drain().then_inc(agg_done[bank], 1)
                if bank == 1:
                    quads.add((slots.value() + QD - 1) // QD)
                    slots.set(0)

            codes(1, 0, PER - 1, SLICES - 1)

            def step(v, b, sums=True):
                j = v * PER + b
                pa = (b + 1) % 2
                pe.wait_ge(code_used[0], j)
                codes(0, j, b, v)
                if sums:
                    aggregate(j - 3, 0, j - 3, pa, (j - 3) * 2 + PARTS - 1)
                pe.wait_ge(code_used[1], j)
                codes(1, j, PER - 1 - b, SLICES - 1 - v)
                if sums:
                    aggregate(TILES + 2 - j, 1, j - 3, pa, (j - 3) * 2 + PARTS)

            step(0, 1, False)
            aggregate(0, 0, 0, 0, None)
            aggregate(TILES - 1, 1, 0, 0, PARTS)
            for b in range(2, PER):
                step(0, b, False)
            with pe.Fori(1, PAIRS // PER) as v:
                for b in range(PER):
                    step(v, b)
            for j in range(PAIRS - 3, PAIRS):
                aggregate(j, 0, j, j % 2, j * 2 + PARTS - 1)
                aggregate(TILES - 1 - j, 1, j, j % 2, j * 2 + PARTS)

            for p in range(PARTS):
                pe.wait_ge(part_done, p + 1)
                pe.transpose(ps_t[:, 0, :], pooled[:], ident[:]).then_inc(part_turned, 1)
            pe.wait_ge(pooledT_ready, 1)
            pe.transpose(ps_t[:, 1, :], pooledT[:], ident[:]).then_inc(pooledT_turned, 1)

            pe.wait_ge(block1_done, PAIRS // LNB)
            for p in range(PARTS):
                mm = pe.matmul(ps_h[:, p, :], to_lane[:, p, :], row1[:, 0, 0:F], start=True, stop=True)
                mm = pe.matmul(ps_t[:, p, 0:TW - F], to_lane[:, p, :], row1[:, 0, F:TW], start=True, stop=True)
            mm.then_inc(ownl_done, 1)
            end.set(0)
            place, first, second = Count(pe, "pe_place"), Count(pe, "pe_first"), Count(pe, "pe_second")

            def weighted(bank, weights, values, start=False):
                return pe.matmul(wsum[bank][:, 0:F + 2], weights, values, start=start, stop=False,
                                 skip_group_check=True)

            def attend(bank, j, entry):
                if not (isinstance(j, int) and j == 0):
                    pe.wait_ge(sum_used, j * 2 + bank - 1)
                pe.wait_ge(own_copied, j * 2 + bank + 1)
                pe.wait_ge(own_ready, j * 2 + bank + 1)
                weighted(bank, own_diag[:, bank, :], ownc[bank][:, 0:F + 2], True)
                entries = range(PARTS) if isinstance(j, int) and j == 0 and bank == 0 else [entry]
                for e in entries:
                    until = end_of(pe, e)
                    with pe.Fori(end.value(FLAT - 4 * GR), until, 2) as s:
                        place.set(s % RINGS)
                        first.set(s + 1)
                        second.set(s + 2)
                        pe.wait_ge(diag_ready, first.value())
                        weighted(bank, diag[:, 0, :], at(got, place.value(RINGS - 2))[:, 0:F + 2]).then_inc(diag_used, 1)
                        pe.wait_ge(diag_ready, second.value())
                        weighted(bank, diag[:, 1, :], at(got, place.value(RINGS - 2) + 1)[:, 0:F + 2]
                                 ).then_inc(used[ATTEND], 1)
                    end.set(until)
                pe.drain().then_inc(sum_done, 1)

            attend(0, 0, None)
            attend(1, 0, PARTS)
            with pe.Fori(1, PAIRS) as j:
                attend(0, j, j * 2 + PARTS - 1)
                attend(1, j, j * 2 + PARTS)

        @block.scalar
        def _(act):
            def load_x(c, i):
                act.dma_start(xs[i], (x[c * HC * P:(c + 1) * HC * P, :] if isinstance(c, int)
                                      else x[bass.ds(c * (HC * P), HC * P), :])
                              .rearrange("(t p) f -> p t f", p=P)).then_inc(x_in[i], 16)

            def copy_xT(c, i):
                act.wait_ge(x_turned, c + 1)
                act.activation(xT[i], ps_t[:], ACT.Copy).then_inc(xT_copied, 1)

            def copy_h(c):
                act.wait_ge(h_done, c + 1)
                dst = rows_sb[:, c * HC:(c + 1) * HC, :] if isinstance(c, int) else rows_sb[:, bass.ds(c * HC, HC), :]
                act.activation(dst, ps_h[:], ACT.Copy).then_inc(h_copied, 1)
                act.wait_ge(h_copied, c + 1)
                act.dma_start(rows(tab_h, c * HC, 1, HC).rearrange("(t p) f -> p t f", p=P), dst
                              ).then_inc(h_saved, 16)

            load_x(0, 0)
            load_x(1, 1)
            act.wait_ge(consts, CONSTS)
            for table in (tab_h, tab0, tab1):
                act.dma_start(table[0:1, :], zeros[0:1, 0:table.shape[1]]).then_inc(zeros_saved, 16)

            act.wait_ge(code_ready[0], 1)
            act.activation(code0[:], code[0][:], ACT.Copy).then_inc(code_used[0], 1)
            act.wait_ge(code_used[0], 1)
            act.dma_start(codes0, code0[:]).then_inc(code0_saved, 16)
            act.wait_ge(code0_saved, 16)
            for p, (n, r) in enumerate(zip(LANES, PART_ROW)):
                act.dma_start(part_code[p][:], codes0[r:r + P // n, :].rearrange("r (l w) -> (r l) w", l=n)
                              ).then_inc(part_in, 16)

            copy_xT(0, 0)
            load_x(2, 0)
            copy_xT(1, 1)
            load_x(3, 1)
            copy_h(0)
            with act.Fori(1, CHUNKS // 2 - 1) as v:
                for i in range(2):
                    c = v * 2 + i
                    copy_xT(c, i)
                    load_x(c + 2, i)
                    copy_h(c - 1)
            for c in (CHUNKS - 2, CHUNKS - 1):
                copy_xT(c, c % 2)
                copy_h(c - 1)
            copy_h(CHUNKS - 1)

            saves = Count(act, "act_saves")
            ids_at[act] = (Count(act, "act_ahead"), Count(act, "act_from"))
            end = Count(act, "act_end")
            from_slot = [Count(act, f"act_from{i}") for i in range(3)]
            told = [[Count(act, f"act_told{i}_{h}") for h in range(2)] for i in range(2)]
            for c in (*told[0], *told[1]):
                c.set(1)
            act.nop().then_inc(list_saved, 1)
            act.nop().then_inc(list_saving, IDS)
            saves.set(1)

            def are_saved(n):
                act.wait_ge(list_saving, saves.value() * IDS)
                act.nop().then_inc(list_saved, n)

            def save_list(entry, heads, loads=()):
                act.wait_ge(list_ready, entry + 1)
                until = end_of(act, entry)
                begin = end.value(FLAT - 4 * GR)
                n = within(until - begin, 2, N)
                for i, h in loads:
                    act.wait_ge(idx_in[SUMS][i][h], told[i][h].value() * IDS)
                act.wait_ge(list_saving, saves.value() * IDS)
                for part in range(2):
                    act.dma_start(lists[part][:, bass.ds(begin, 2 * GR)],
                                  heads[part * HP:(part + 1) * HP, :]).then_inc(list_saving, 16)
                saves.add()
                with act.If(n > GR):
                    act.wait_ge(list_saving, saves.value() * IDS)
                    with act.Fori(GR, n + GR, GR) as q:
                        to = within(begin + q, 0, FLAT - 2 * GR)
                        for part in range(2):
                            act.dma_start(lists[part][:, bass.ds(to, GR)],
                                          list_sb[part * HP:(part + 1) * HP, bass.ds(q, GR)]).then_inc(list_saving, 16)
                        saves.add()
                    act.nop()
                act.nop()
                end.set(until)

            def first_ids(pa):
                act.wait_ge(used[SUMS], from_slot[0].value() // 2 + CREDIT)
                begin, until = from_slot[1].value(FLAT - 4 * GR), from_slot[2].value(FLAT - 4 * GR)
                load_ids(act, SUMS, pa, begin, within(until - begin, 4, FLAT), others=False, told=told)

            def other_ids(pa, of=0):
                begin, until = from_slot[of].value(FLAT - 4 * GR), from_slot[of + 1].value(FLAT - 4 * GR)
                load_ids(act, SUMS, pa, begin, within(until - begin, 4, FLAT), first=False, told=told)

            def next_pair():
                for i in range(2):
                    from_slot[i].set(from_slot[i + 1].value())
                from_slot[2].set(end.value())

            def relu(t, bank, j):
                act.wait_ge(agg_done[bank], j + 1)
                act.activation(at(rows_sb, t), agg[bank][:], ACT.Relu).then_inc(relu_done[bank], 1)
                act.wait_ge(relu_done[bank], j + 1)
                act.dma_start(rows(tab0, t, 1), at(rows_sb, t)).then_inc(tab0_saved, 16)

            for p in range(PARTS + 1):
                save_list(p, head[p % 2])
                are_saved(1)
            next_pair()
            first_ids(0)

            def relus(j):
                relu(j, 0, j)
                relu(TILES - 1 - j, 1, j)

            def step(j, pa, sums=True, ids=True, others=True):
                if sums:
                    relu(j - 3, 0, j - 3)
                if ids:
                    first_ids(1 - pa)
                if sums:
                    relu(TILES + 2 - j, 1, j - 3)
                save_list(j * 2 + PARTS - 1, head[(PARTS - 1) % 2], [(i, h) for i in range(2) for h in range(2)])
                are_saved(1)
                save_list(j * 2 + PARTS, head[PARTS % 2])
                are_saved(1)
                if others:
                    other_ids(pa)
                next_pair()

            other_ids(0, 1)
            step(1, 1, False, False, False)
            step(2, 0, False, others=False)
            step(3, 1)
            with act.Fori(2, PAIRS // 2) as v:
                for pa in range(2):
                    step(v * 2 + pa, pa)
            relu(PAIRS - 3, 0, PAIRS - 3)
            first_ids(1)
            relu(TILES + 2 - PAIRS, 1, PAIRS - 3)
            other_ids(0)
            next_pair()
            relus(PAIRS - 2)
            other_ids(1)
            relus(PAIRS - 1)
            for part in range(2):
                act.dma_start(lists[part][:, bass.ds(end.value(FLAT - 4 * GR), 2 * GR)], zids[0:HP, :]
                              ).then_inc(ends_saved, 16)

            def save_blocks(a, table, src, done, saved, ahead):
                act.wait_ge(done, a + 1)
                for t in (a * LNB, TILES - LNB - a * LNB):
                    if isinstance(t, int):
                        part = src[:, t:t + LNB, :]
                    else:
                        part = src[:, bass.ds(t, LNB), :]
                    act.dma_start(rows(table, t, ahead, LNB).rearrange("(t p) w -> p t w", p=P), part
                                  ).then_inc(saved, 16)

            for a in range(PAIRS // LNB):
                save_blocks(a, tab1, row1, block1_done, tab1_saved, 1)

            sets = Count(act, "act_sets")
            act.nop().then_inc(score_used, 1)
            end.set(0)

            def exponentials(s, pairs, spread):
                n = 2 * pairs
                sets.add()
                lasts = (last0, last1, last2, last3)
                for i in range(pairs):
                    lasts[2 * i].set((s + 2 * i) // 2 + 1)
                    lasts[2 * i + 1].set((s + 2 * i) // 2 + CREDIT)
                act.drain()
                act.wait_ge(score_ready, sets.value())
                act.activation(expo[:, 0:n], score[:, 0:n], ACT.Exp, bias=shift[:, 0:1]).then_inc(score_used, 1)
                act.drain()
                for i in range(n):
                    act.wait_ge(used[ATTEND] if i % 2 else diag_used, lasts[i].value())
                    act.activation(diag[:, i % 2, :], spread, ACT.Copy, scale=expo[:, i:i + 1]).then_inc(diag_ready, 1)

            def attend(bank, j, entry):
                part0 = isinstance(j, int) and j == 0 and bank == 0
                if not (isinstance(j, int) and j == 0):
                    act.wait_ge(sum_done, j * 2 + bank - 1)
                t = j if bank == 0 else TILES - 1 - j
                weight = own_expo[:, t:t + 1] if isinstance(t, int) else own_expo[:, bass.ds(t, 1)]
                act.activation(own_diag[:, bank, :], ident[:], ACT.Copy, scale=weight).then_inc(own_ready, 1)
                for e in (range(PARTS) if part0 else [entry]):
                    until = end_of(act, e)
                    spread = to_row[:, e, :] if part0 else ident[:]
                    by_four(act, end, until, lambda s, pairs: exponentials(s, pairs, spread))

            last0, last1, last2, last3 = (Count(act, f"act_last{i}") for i in range(4))
            act.wait_ge(params, 2)
            act.wait_ge(own_scored, 1)
            act.activation(own_expo[:], own_score[:], ACT.Exp, bias=shift[:, 0:1])
            act.drain()
            attend(0, 0, None)
            attend(1, 0, PARTS)
            with act.Fori(1, LNB) as j:
                attend(0, j, j * 2 + PARTS - 1)
                attend(1, j, j * 2 + PARTS)
            with act.Fori(1, PAIRS // LNB) as a:
                save_blocks(a - 1, out, rows_sb, block2_done, out_saved, 0)
                with act.Fori(a * LNB, a * LNB + LNB) as j:
                    attend(0, j, j * 2 + PARTS - 1)
                    attend(1, j, j * 2 + PARTS)
            save_blocks(PAIRS // LNB - 1, out, rows_sb, block2_done, out_saved, 0)

        @block.vector
        def _(dve):
            dve.memset(cnt[:], 0.0)
            dve.memset(cnt_m[:], 0.0)
            dve.memset(ofs[0:1, 0:1], 0)
            for i in range(2):
                dve.memset(head[i][:], 0)
            for _ in range(CREDIT):
                dve.nop().then_inc(used[MAXIMA], 1)
            dve.wait_ge(loaded, 48)
            dve.tensor_scalar(den[:, 0:1], beta_sb[:], -1.0, None, ALU.mult)
            dve.drain()
            dve.tensor_tensor(shift[:], beta_sb[:], den[:, 0:1], ALU.min).then_inc(params, 1)
            dve.wait_ge(consts, CONSTS)
            for p, n in enumerate((*LANES, 1)):
                dve.tensor_scalar(lane[:, p:p + 1], lane[:, p:p + 1], n - 1, None, ALU.bitwise_and)
                dve.drain()
                dve.tensor_scalar(first_col[:, p:p + 1], lane[:, p:p + 1], float(SLICE // n), None, ALU.mult)
                dve.drain()
            dve.nop().then_inc(params, 1)

            flat = cand[:].rearrange("p c s -> p (c s)")

            def take_columns(codes, h, remove):
                eight = slice(8 * h, 8 * h + 8)
                dve.max(top[:, eight], codes)
                dve.drain()
                dve.max_index(col[:, eight], top[:, eight], codes)
                dve.drain()
                if remove:
                    drop_columns(codes, h)

            def drop_columns(codes, h):
                dve.match_replace(codes, top[:, 8 * h:8 * h + 8], codes, 0.0)
                dve.drain()

            def expand(part):
                dve.tensor_copy(topi[:], top[:])
                dve.tensor_scalar(colf[:], col[:], first_col[:, part:part + 1], None, ALU.add)
                dve.drain()
                dve.tensor_tensor(cand[:], colf[:].rearrange("p (c a) -> p c a", a=1).to_broadcast([P, COLS, SLICES]),
                                  base[:].rearrange("p (a s) -> p a s", a=1).to_broadcast([P, COLS, SLICES]), ALU.add)
                dve.tensor_tensor(bits[:], topi[:].rearrange("p (c a) -> p c a", a=1).to_broadcast([P, COLS, SLICES]),
                                  bit[:].rearrange("p (a s) -> p a s", a=1).to_broadcast([P, COLS, SLICES]),
                                  ALU.bitwise_and)
                dve.drain()
                dve.scalar_tensor_tensor(cand[:], bits[:], 0.0, cand[:], ALU.is_gt, ALU.mult)
                dve.drain()
                dve.tensor_scalar(is_set[:, 0:COLS * SLICES], flat, 0.0, 0.0, ALU.is_gt, ALU.add,
                                  accum_out=cnt[:, 1:2])
                dve.drain()

            def most_of_rows():
                dve.transpose(cnt_t[:], cnt[:])
                dve.drain()
                dve.tensor_reduce(cnt_m[:, 0:1], cnt_t[:], AX.X, ALU.max)
                dve.drain()
                dve.transpose(cnt_u[:], cnt_m[:])
                dve.drain()
                for b in range(4):
                    dve.tensor_copy(cnt_q[0:1, b, :], cnt_u[32 * b:32 * b + 1, 0:2])
                dve.drain()
                dve.tensor_reduce(most[0:1, :], cnt_q[0:1].rearrange("p b c -> p c b"), AX.X, ALU.max)
                dve.drain()
                dve.tensor_copy(mosti[0:1, 0:2], most[0:1, :])
                dve.tensor_tensor(mosti[0:1, 2:3], most[0:1, 0:1], most[0:1, 1:2], ALU.max)
                dve.drain()

            def emit(to):
                dve.max(best[:], flat)
                dve.drain()
                dve.tensor_copy(to, best[:])
                dve.match_replace(flat, best[:], flat, 0.0)
                dve.drain()

            slot = Count(dve, "dve_slot")

            def emit_more():
                emit(list_sb[:, bass.ds(slot.value(N), 8)])
                slot.add(8)
                dve.tensor_scalar(length[:], length[:], 8.0, None, ALU.add)
                dve.drain()

            def zeros_behind():
                dve.tensor_copy(list_sb[:, bass.ds(slot.value(N), 2 * GR)], zids[:])

            def extract(entry, part, codes, heads, after=None):
                def more():
                    dve.wait_ge(list_saved, entry + 1)
                    dve.tensor_scalar(length[:], length[:], 0.0, float(COLS), ALU.mult, ALU.add)
                    dve.drain()

                dve.tensor_scalar(is_set[:, 0:codes.shape[1]], codes, 0.0, 0.0, ALU.is_gt, ALU.add,
                                  accum_out=cnt[:, 0:1])
                take_columns(codes, 0, True)
                take_columns(codes, 1, False)
                expand(part)
                most_of_rows()
                if not isinstance(entry, int) or entry >= 2:
                    dve.wait_ge(list_saved, entry)
                dve.tensor_scalar(lengthi[:], most[0:1, 1:2], SHORTEST - 1.0, 1.0, ALU.max, ALU.add)
                dve.drain()
                dve.tensor_scalar(lengthi[:], lengthi[:], 1, 1, ALU.logical_shift_right, ALU.logical_shift_left)
                emit(heads[:, 0:8])
                dve.tensor_copy(length[:], lengthi[:])
                emit(heads[:, 8:COLS])
                both = dve.value_load(mosti[0:1, 2:3], min_val=0, max_val=N)
                with dve.If(both > COLS):
                    columns = dve.value_load(mosti[0:1, 0:1], min_val=0, max_val=N)
                    entries = dve.value_load(mosti[0:1, 1:2], min_val=0, max_val=N)
                    slot.set(COLS)
                    with dve.If(entries > COLS):
                        more()
                        with dve.Fori(COLS, entries, 8):
                            emit_more()
                        zeros_behind()
                        dve.drain()
                    dve.nop()
                    with dve.If(columns > COLS):
                        with dve.If(entries <= COLS):
                            more()
                        dve.nop()
                        drop_columns(codes, 1)
                        with dve.Fori(COLS, columns, COLS):
                            take_columns(codes, 0, True)
                            take_columns(codes, 1, True)
                            expand(part)
                            most_of_rows()
                            ids = dve.value_load(mosti[0:1, 1:2], min_val=0, max_val=N)
                            with dve.Fori(0, ids, 8):
                                emit_more()
                            dve.nop()
                        zeros_behind()
                        dve.drain()
                    dve.nop()
                dve.nop()
                this, next_ = ((ofs[0:1, entry:entry + 1], ofs[0:1, entry + 1:entry + 2]) if isinstance(entry, int)
                               else (ofs[0:1, bass.ds(entry, 1)], ofs[0:1, bass.ds(entry + 1, 1)]))
                dve.drain()
                dve.tensor_tensor(next_, this, length[:], ALU.add)
                if after is not None:
                    dve.drain().then_inc(after, 1)
                    dve.nop().then_inc(list_ready, 1)
                else:
                    dve.drain().then_inc(list_ready, 1)

            dve.wait_ge(part_in, 16 * PARTS)
            for p in range(PARTS):
                extract(p, p, part_code[p][:], head[p % 2])
            dve.wait_ge(code_ready[1], 1)
            extract(PARTS, PARTS, code[1][:], head[PARTS % 2], code_used[1])
            with dve.Fori(1, PAIRS) as j:
                for bank in range(2):
                    dve.wait_ge(code_ready[bank], j + 1)
                    extract(j * 2 + PARTS - 1 + bank, PARTS, code[bank][:], head[(PARTS - 1 + bank) % 2],
                            code_used[bank])

            def rsqrt(y, v, a, b):
                dve.tensor_scalar(a.bitcast(i32), v.bitcast(i32), 1, None, ALU.logical_shift_right)
                dve.drain()
                dve.tensor_scalar(y.bitcast(i32), a.bitcast(i32), -1.0, float(0x5F3759DF), ALU.mult, ALU.add)
                dve.drain()
                for _ in range(4):
                    dve.tensor_tensor(a, y, y, ALU.mult)
                    dve.drain()
                    dve.scalar_tensor_tensor(b, a, -0.5, v, ALU.mult, ALU.mult)
                    dve.drain()
                    dve.scalar_tensor_tensor(y, b, 1.5, y, ALU.add, ALU.mult)
                    dve.drain()

            T = 2 * LNB

            def tile_of(a, k):
                return (a * LNB + k) if k < LNB else (TILES - LNB - a * LNB + k - LNB)

            def normalise(buf, a):
                dve.drain()
                for k in range(T):
                    dve.bn_stats(stats[:, k, :], at(buf, tile_of(a, k))[:, 0:F])
                dve.drain()
                for k in range(T):
                    dve.bn_aggr(mv[:, k, :], stats[:, k, :])
                dve.drain()
                dve.tensor_scalar(nw[:, 0, :], mv[:, :, 1], LN_EPS, None, ALU.add)
                dve.drain()
                rsqrt(nw[:, 1, :], nw[:, 0, :], nw[:, 2, :], nw[:, 3, :])
                for k in range(T):
                    row = at(buf, tile_of(a, k))[:, 0:F]
                    dve.tensor_scalar(row, row, mv[:, k, 0:1], nw[:, 1, k:k + 1], ALU.subtract, ALU.mult)
                dve.drain()

            end = Count(dve, "dve_end")

            def maximum(entry):
                dve.memset(most2[:], 0.0)
                dve.drain()
                until = end_of(dve, entry)
                with dve.Fori(end.value(FLAT - 4 * GR), until, 2) as s:
                    dve.wait_ge(landed[MAXIMA], s // QD + LAG + 1)
                    dve.tensor_tensor(most2[:], most2[:], got[:, bass.ds(s % RINGS, 2), 0:F], ALU.max
                                      ).then_inc(used[MAXIMA], 1)
                    dve.drain()
                end.set(until)
                dve.tensor_tensor(pooled[:], most2[:, 0, :], most2[:, 1, :], ALU.max)

            def add_maximum(t, of=pooled):
                dve.drain()
                dve.tensor_tensor(pooled[:], of[:] if of is pooled else of, at(rows_sb, t), ALU.max)
                dve.drain()
                row = at(row1, t)[:, 0:F]
                dve.tensor_tensor(row, row, pooled[:], ALU.add)

            for p, (n, r) in enumerate(zip(LANES, PART_ROW)):
                maximum(p)
                dve.drain().then_inc(part_done, 1)
                dve.wait_ge(part_turned, p + 1)
                dve.tensor_reduce(pooledT[:, r:r + P // n], ps_t[:, 0, :].rearrange("f (r l) -> f r l", l=n),
                                  AX.X, ALU.max)
                dve.drain()
            dve.nop().then_inc(pooledT_ready, 1)
            dve.wait_ge(pooledT_turned, 1)
            dve.wait_ge(x_again, 64)
            for i in range(2):
                dve.wait_ge(relu_done[i], PAIRS)
            dve.wait_ge(list_saved, ENTRIES + 1)
            add_maximum(0, ps_t[:, 1, :])
            maximum(PARTS)
            add_maximum(TILES - 1)

            def pair_of_maxima(j):
                maximum(j * 2 + PARTS - 1)
                add_maximum(j)
                maximum(j * 2 + PARTS)
                add_maximum(TILES - 1 - j)

            def finish_layer0(a):
                normalise(row1, a)
                for k in range(T):
                    row = at(row1, tile_of(a, k))[:, 0:F]
                    dve.scalar_tensor_tensor(squares[:, k, :], row, 1.0, row, ALU.mult, ALU.mult,
                                             accum_out=nw[:, 4, k:k + 1])
                dve.drain()
                rsqrt(nw[:, 1, :], nw[:, 4, :], nw[:, 2, :], nw[:, 3, :])
                for half in range(2):
                    t = tile_of(a, half * LNB)
                    some = row1[:, t:t + LNB, :] if isinstance(t, int) else row1[:, bass.ds(t, LNB), :]
                    k = slice(half * LNB, half * LNB + LNB)
                    dve.tensor_tensor(some[:, :, F], nw[:, 4, k], nw[:, 1, k], ALU.mult)
                    dve.memset(some[:, :, F + 1:TW], 1.0) if isinstance(t, int) else \
                        dve.tensor_scalar(some[:, :, F + 1:TW], some[:, :, 0:TW - F - 1], 0.0, 1.0, ALU.mult, ALU.add)
                dve.drain().then_inc(block1_done, 1)

            with dve.Fori(1, LNB) as j:
                pair_of_maxima(j)
            finish_layer0(0)
            with dve.Fori(1, PAIRS // LNB) as a:
                with dve.Fori(0, LNB) as k:
                    pair_of_maxima(a * LNB + k)
                finish_layer0(a)

            end.set(0)
            sets = Count(dve, "dve_sets")
            dve.wait_ge(ownl_done, 1)
            for p in range(PARTS):
                dve.tensor_copy(ownl[:, p, 0:F], ps_h[:, p, :])
                dve.tensor_copy(ownl[:, p, F:TW], ps_t[:, p, 0:TW - F])
            dve.drain()

            def own_row(t, bank):
                dve.drain()
                dve.tensor_copy(ownc[bank][:], at(row1, t))
                dve.drain().then_inc(own_copied, 1)

            norms = row1[:, :, F]
            dve.tensor_tensor(own_score[:], norms, norms, ALU.mult)
            dve.drain()
            dve.tensor_scalar(own_den[:], own_score[:], COS_EPS, None, ALU.add)
            dve.drain()
            dve.reciprocal(own_den[:], own_den[:])
            dve.drain()
            dve.scalar_tensor_tensor(own_score[:], own_score[:], beta_sb[:, 0:1], own_den[:], ALU.mult, ALU.mult
                                     ).then_inc(own_scored, 1)

            places = [Count(dve, f"dve_place{i}") for i in range(2)]
            quad = Count(dve, "dve_quad")

            def some_scores(s, pairs, own):
                n = 2 * pairs
                for i in range(pairs):
                    places[i].set((s + 2 * i) % RINGS)
                quad.set((s + n - 2) // QD + LAG + 1)
                dve.drain()
                dve.wait_ge(landed[ATTEND], quad.value())
                for i in range(pairs):
                    pair = got[:, bass.ds(places[i].value(RINGS - 2), 2), :]
                    for k in range(2):
                        dve.scalar_tensor_tensor(prod[:, 2 * i + k, :], pair[:, k, 0:F], 1.0, own[:, 0:F],
                                                 ALU.mult, ALU.mult, accum_out=dots[:, 2 * i + k:2 * i + k + 1])
                    dve.tensor_scalar(den[:, 2 * i:2 * i + 2], pair[:, :, F], own[:, F:F + 1], COS_EPS,
                                      ALU.mult, ALU.add)
                dve.drain()
                dve.reciprocal(den[:, 0:n], den[:, 0:n])
                sets.add()
                dve.drain()
                dve.wait_ge(score_used, sets.value())
                dve.scalar_tensor_tensor(score[:, 0:n], dots[:, 0:n], beta_sb[:, 0:1], den[:, 0:n],
                                         ALU.mult, ALU.mult).then_inc(score_ready, 1)

            def scores(entry, own):
                until = end_of(dve, entry)
                by_four(dve, end, until, lambda s, pairs: some_scores(s, pairs, own))

            def finish(t, bank, n):
                dve.wait_ge(sum_done, n + 1)
                dve.reciprocal(nw[:, 5, bank:bank + 1], wsum[bank][:, F + 1:F + 2])
                dve.drain()
                row = at(rows_sb, t)
                dve.scalar_tensor_tensor(row, wsum[bank][:, 0:F], nw[:, 5, bank:bank + 1], ownc[bank][:, 0:F],
                                         ALU.mult, ALU.add).then_inc(sum_used, 1)

            own_row(0, 0)
            for p in range(PARTS):
                scores(p, ownl[:, p, :])
            own_row(TILES - 1, 1)
            scores(PARTS, ownc[1])
            finish(0, 0, 0)

            def pair_of_tiles(j, first=False):
                own_row(j, 0)
                scores(j * 2 + PARTS - 1, ownc[0])
                if not first:
                    finish(TILES - j, 1, j * 2 - 1)
                own_row(TILES - 1 - j, 1)
                scores(j * 2 + PARTS, ownc[1])
                finish(j, 0, j * 2)

            def finish_layer1(a):
                j = a * LNB + LNB - 1
                finish(TILES - 1 - j, 1, j * 2 + 1)
                normalise(rows_sb, a)
                dve.nop().then_inc(block2_done, 1)

            with dve.Fori(1, LNB) as j:
                pair_of_tiles(j)
            finish_layer1(0)
            with dve.Fori(1, PAIRS // LNB) as a:
                pair_of_tiles(a * LNB, True)
                with dve.Fori(1, LNB) as k:
                    pair_of_tiles(a * LNB + k)
                finish_layer1(a)


_INS = ["x", "adj", "L0_gnn_weight", "L0_gnn_bias", "L1_gnn_beta"]


def kernel(**inputs):
    import concourse.bacc as bacc
    from concourse.bass_utils import run_bass_kernel_spmd as run

    nc = bacc.Bacc("TRN2", target_bir_lowering=False, num_devices=1)
    arrays = {n: np.ascontiguousarray(inputs[n]) for n in _INS}
    args = [nc.dram_tensor(f"in_{n}", a.shape, mybir.dt.from_np(a.dtype), kind="ExternalInput").ap()
            for n, a in arrays.items()]
    out = nc.dram_tensor("out", inputs["x"].shape, mybir.dt.float32, kind="ExternalOutput").ap()
    adj_resnorm_program(nc, *args, out)
    r = run(nc, [{f"in_{n}": a for n, a in arrays.items()}], core_ids=[0])
    return r.results[0]["out"]
```
